# Optimizing a Trainium2 kernel written in Bass

```python
import numpy as np
import jax
import jax.numpy as jnp

def _softmax(x, axis=-1):
    return jax.nn.softmax(x, axis=axis)

def _gelu(x):
    return jax.nn.gelu(x, approximate=True)

def _silu(x):
    return jax.nn.silu(x)

def _sigmoid(x):
    return jax.nn.sigmoid(x)

def _layernorm(x, axis=-1, eps=1e-05):
    m = jnp.mean(x, axis=axis, keepdims=True)
    v = jnp.var(x, axis=axis, keepdims=True)
    return (x - m) / jnp.sqrt(v + eps)

def _scatter_add(tgt, idx, src, axis=0):
    return tgt.at[idx].add(src)

def _segment_sum(src, seg, n):
    return jax.ops.segment_sum(src, seg, n)
kernel_name = 'mk_hybrid_d1_jaxref_r4_0dde1c'

def setup_inputs(seed: int=0):
    np.random.seed(seed)
    _w = jnp.asarray

    def _L0_attn_a_setup():
        import jax, jax.numpy as jnp
        import numpy as np
        HID = 256
        NH = 16
        NKV = 4
        HD = 64
        C = 64
        RATIO = 0.125
        KS = 7

        def _block_causal_attention(x, qw, kw, vw, ow, k):
            B, nc, _, D = x.shape
            T = nc * k
            xf = x.reshape(B, T, D)
            q = (xf @ qw.T).reshape(B, T, NH, HD).transpose(0, 2, 1, 3)
            kk = (xf @ kw.T).reshape(B, T, NKV, HD).transpose(0, 2, 1, 3)
            v = (xf @ vw.T).reshape(B, T, NKV, HD).transpose(0, 2, 1, 3)
            rep = NH // NKV
            kk = jnp.repeat(kk, rep, axis=1)
            v = jnp.repeat(v, rep, axis=1)
            chunk_ids = jnp.arange(T) // k
            mask = chunk_ids[:, None] >= chunk_ids[None, :]
            scores = jnp.einsum('bhqd,bhkd->bhqk', q, kk) / np.float32(np.sqrt(HD))
            scores = jnp.where(mask[None, None], scores, jnp.finfo(scores.dtype).min)
            p = jax.nn.softmax(scores, axis=-1)
            o = jnp.einsum('bhqk,bhkd->bhqd', p, v)
            o = o.transpose(0, 2, 1, 3).reshape(B, T, NH * HD)
            return (o @ ow.T).reshape(B, nc, k, D)

        def _causal_conv(x, dw, pw):
            B, nc, L, D = x.shape
            xc = x.reshape(B * nc, L, D).transpose(0, 2, 1)
            xp = jnp.pad(xc, ((0, 0), (0, 0), (KS - 1, 0)))
            y = jax.lax.conv_general_dilated(xp, dw, window_strides=(1,), padding='VALID', dimension_numbers=('NCH', 'OIH', 'NCH'), feature_group_count=D)
            y = jax.nn.gelu(y, approximate=False)
            y = jnp.einsum('ncl,oc->nol', y, pw)
            return y.transpose(0, 2, 1).reshape(B, nc, L, D)

        def _forward(hidden_states, q_w, k_w, v_w, o_w, dw_r, pw_r, dw_i, pw_i, gate_w, alpha_raw):
            B, N, D = hidden_states.shape
            pad_len = -N % C
            x = jnp.pad(hidden_states, ((0, 0), (0, pad_len), (0, 0))) if pad_len else hidden_states
            nc = x.shape[1] // C
            chunks = x.reshape(B, nc, C, D)
            Xh = jnp.fft.rfft(chunks.astype(jnp.float32), axis=2)
            M = Xh.shape[2]
            k = max(1, int(M * RATIO))
            X_low, X_high = (Xh[:, :, :k, :], Xh[:, :, k:, :])
            A_r = _block_causal_attention(X_low.real, q_w, k_w, v_w, o_w, k)
            A_i = _block_causal_attention(X_low.imag, q_w, k_w, v_w, o_w, k)
            A_low = jax.lax.complex(A_r, A_i)
            H_r = _causal_conv(X_high.real, dw_r, pw_r)
            H_i = _causal_conv(X_high.imag, dw_i, pw_i)
            g = jax.nn.sigmoid(chunks.mean(axis=2) @ gate_w.T)[:, :, None, :]
            A_high = jax.lax.complex(H_r * g, H_i * g) + X_high
            alpha = jax.nn.sigmoid(alpha_raw)
            A_low_fused = alpha * A_low + (1.0 - alpha) * X_low
            Y_hat = jnp.concatenate([A_low_fused, A_high], axis=2)
            Y = jnp.fft.irfft(Y_hat, n=C, axis=2)
            return Y.reshape(B, -1, D)[:, :N, :].astype(hidden_states.dtype)
        key = jax.random.key(seed)
        ks = jax.random.split(key, 11)
        B, N = (4, 1024)
        s = 0.02
        return {'hidden_states': jax.random.normal(ks[0], (B, N, HID), jnp.float32), 'q_w': jax.random.normal(ks[1], (NH * HD, HID), jnp.float32) * s, 'k_w': jax.random.normal(ks[2], (NKV * HD, HID), jnp.float32) * s, 'v_w': jax.random.normal(ks[3], (NKV * HD, HID), jnp.float32) * s, 'o_w': jax.random.normal(ks[4], (HID, NH * HD), jnp.float32) * s, 'dw_r': jax.random.normal(ks[5], (HID, 1, KS), jnp.float32) * 0.3, 'pw_r': jax.random.normal(ks[6], (HID, HID), jnp.float32) * s, 'dw_i': jax.random.normal(ks[7], (HID, 1, KS), jnp.float32) * 0.3, 'pw_i': jax.random.normal(ks[8], (HID, HID), jnp.float32) * s, 'gate_w': jax.random.normal(ks[9], (HID, HID), jnp.float32) * s, 'alpha_raw': jnp.zeros((1,), jnp.float32)}
    _L0_attn_a_in = _L0_attn_a_setup()

    def _L0_attn_b_setup():
        import jax, jax.numpy as jnp
        import numpy as np
        MAX_POSITION = 1024
        EMBED_DIM = 256
        NUM_HEADS = 16
        HEAD_DIM = EMBED_DIM // NUM_HEADS
        B, S = (2, 512)
        key = jax.random.key(seed)
        ks = jax.random.split(key, 6)
        scale_in = 1.0 / np.sqrt(EMBED_DIM)
        return {'x': jax.random.normal(ks[0], (B, S, EMBED_DIM), dtype=jnp.float32), 'W_in': jax.random.normal(ks[1], (EMBED_DIM, 3 * EMBED_DIM), dtype=jnp.float32) * scale_in, 'b_in': jnp.zeros((3 * EMBED_DIM,), dtype=jnp.float32), 'W_out': jax.random.normal(ks[2], (EMBED_DIM, EMBED_DIM), dtype=jnp.float32) * scale_in, 'b_out': jnp.zeros((EMBED_DIM,), dtype=jnp.float32), 'rel_emb': jax.random.normal(ks[3], (MAX_POSITION, NUM_HEADS), dtype=jnp.float32) * 0.02}
    _L0_attn_b_in = _L0_attn_b_setup()

    def _L0_ffn_setup():
        import jax, jax.numpy as jnp
        import numpy as np
        B, S, D, O, E, K = (4, 512, 256, 256, 8, 2)
        key = jax.random.key(seed)
        ks = jax.random.split(key, 5)
        scale_in = 1.0 / np.sqrt(D)
        x = jax.random.normal(ks[0], (B, S, D), dtype=jnp.float32)
        gate_w = jax.random.uniform(ks[1], (E, D), jnp.float32, -scale_in, scale_in)
        gate_b = jax.random.uniform(ks[2], (E,), jnp.float32, -scale_in, scale_in)
        expert_w = jax.random.uniform(ks[3], (E, D, O), jnp.float32, -scale_in, scale_in)
        expert_b = jax.random.uniform(ks[4], (E, O), jnp.float32, -scale_in, scale_in)
        return {'x': x, 'gate_w': gate_w, 'gate_b': gate_b, 'expert_w': expert_w, 'expert_b': expert_b}
    _L0_ffn_in = _L0_ffn_setup()
    _d = {'L0_attn_a_hidden_states': _L0_attn_a_in['hidden_states'], 'L0_attn_a_q_w': _L0_attn_a_in['q_w'], 'L0_attn_a_k_w': _L0_attn_a_in['k_w'], 'L0_attn_a_v_w': _L0_attn_a_in['v_w'], 'L0_attn_a_o_w': _L0_attn_a_in['o_w'], 'L0_attn_a_dw_r': _L0_attn_a_in['dw_r'], 'L0_attn_a_pw_r': _L0_attn_a_in['pw_r'], 'L0_attn_a_dw_i': _L0_attn_a_in['dw_i'], 'L0_attn_a_pw_i': _L0_attn_a_in['pw_i'], 'L0_attn_a_gate_w': _L0_attn_a_in['gate_w'], 'L0_attn_a_alpha_raw': _L0_attn_a_in['alpha_raw'], 'L0_attn_b_W_in': _L0_attn_b_in['W_in'], 'L0_attn_b_b_in': _L0_attn_b_in['b_in'], 'L0_attn_b_W_out': _L0_attn_b_in['W_out'], 'L0_attn_b_b_out': _L0_attn_b_in['b_out'], 'L0_attn_b_rel_emb': _L0_attn_b_in['rel_emb'], 'L0_ffn_gate_w': _L0_ffn_in['gate_w'], 'L0_ffn_gate_b': _L0_ffn_in['gate_b'], 'L0_ffn_expert_w': _L0_ffn_in['expert_w'], 'L0_ffn_expert_b': _L0_ffn_in['expert_b']}
    _x0 = _d['L0_attn_a_hidden_states']
    _d['L0_attn_a_hidden_states'] = jax.random.normal(jax.random.fold_in(jax.random.key(seed), 1), (16, 512, 256), dtype=_x0.dtype)
    del _x0
    return _d

def reference(L0_attn_a_hidden_states, L0_attn_a_q_w, L0_attn_a_k_w, L0_attn_a_v_w, L0_attn_a_o_w, L0_attn_a_dw_r, L0_attn_a_pw_r, L0_attn_a_dw_i, L0_attn_a_pw_i, L0_attn_a_gate_w, L0_attn_a_alpha_raw, L0_attn_b_W_in, L0_attn_b_b_in, L0_attn_b_W_out, L0_attn_b_b_out, L0_attn_b_rel_emb, L0_ffn_gate_w, L0_ffn_gate_b, L0_ffn_expert_w, L0_ffn_expert_b):

    def _L0_attn_a_ref(hidden_states, q_w, k_w, v_w, o_w, dw_r, pw_r, dw_i, pw_i, gate_w, alpha_raw):
        import jax, jax.numpy as jnp
        import numpy as np
        HID = 256
        NH = 16
        NKV = 4
        HD = 64
        C = 64
        RATIO = 0.125
        KS = 7

        def _block_causal_attention(x, qw, kw, vw, ow, k):
            B, nc, _, D = x.shape
            T = nc * k
            xf = x.reshape(B, T, D)
            q = (xf @ qw.T).reshape(B, T, NH, HD).transpose(0, 2, 1, 3)
            kk = (xf @ kw.T).reshape(B, T, NKV, HD).transpose(0, 2, 1, 3)
            v = (xf @ vw.T).reshape(B, T, NKV, HD).transpose(0, 2, 1, 3)
            rep = NH // NKV
            kk = jnp.repeat(kk, rep, axis=1)
            v = jnp.repeat(v, rep, axis=1)
            chunk_ids = jnp.arange(T) // k
            mask = chunk_ids[:, None] >= chunk_ids[None, :]
            scores = jnp.einsum('bhqd,bhkd->bhqk', q, kk) / np.float32(np.sqrt(HD))
            scores = jnp.where(mask[None, None], scores, jnp.finfo(scores.dtype).min)
            p = jax.nn.softmax(scores, axis=-1)
            o = jnp.einsum('bhqk,bhkd->bhqd', p, v)
            o = o.transpose(0, 2, 1, 3).reshape(B, T, NH * HD)
            return (o @ ow.T).reshape(B, nc, k, D)

        def _causal_conv(x, dw, pw):
            B, nc, L, D = x.shape
            xc = x.reshape(B * nc, L, D).transpose(0, 2, 1)
            xp = jnp.pad(xc, ((0, 0), (0, 0), (KS - 1, 0)))
            y = jax.lax.conv_general_dilated(xp, dw, window_strides=(1,), padding='VALID', dimension_numbers=('NCH', 'OIH', 'NCH'), feature_group_count=D)
            y = jax.nn.gelu(y, approximate=False)
            y = jnp.einsum('ncl,oc->nol', y, pw)
            return y.transpose(0, 2, 1).reshape(B, nc, L, D)

        def _forward(hidden_states, q_w, k_w, v_w, o_w, dw_r, pw_r, dw_i, pw_i, gate_w, alpha_raw):
            B, N, D = hidden_states.shape
            pad_len = -N % C
            x = jnp.pad(hidden_states, ((0, 0), (0, pad_len), (0, 0))) if pad_len else hidden_states
            nc = x.shape[1] // C
            chunks = x.reshape(B, nc, C, D)
            Xh = jnp.fft.rfft(chunks.astype(jnp.float32), axis=2)
            M = Xh.shape[2]
            k = max(1, int(M * RATIO))
            X_low, X_high = (Xh[:, :, :k, :], Xh[:, :, k:, :])
            A_r = _block_causal_attention(X_low.real, q_w, k_w, v_w, o_w, k)
            A_i = _block_causal_attention(X_low.imag, q_w, k_w, v_w, o_w, k)
            A_low = jax.lax.complex(A_r, A_i)
            H_r = _causal_conv(X_high.real, dw_r, pw_r)
            H_i = _causal_conv(X_high.imag, dw_i, pw_i)
            g = jax.nn.sigmoid(chunks.mean(axis=2) @ gate_w.T)[:, :, None, :]
            A_high = jax.lax.complex(H_r * g, H_i * g) + X_high
            alpha = jax.nn.sigmoid(alpha_raw)
            A_low_fused = alpha * A_low + (1.0 - alpha) * X_low
            Y_hat = jnp.concatenate([A_low_fused, A_high], axis=2)
            Y = jnp.fft.irfft(Y_hat, n=C, axis=2)
            return Y.reshape(B, -1, D)[:, :N, :].astype(hidden_states.dtype)
        return _forward(hidden_states, q_w, k_w, v_w, o_w, dw_r, pw_r, dw_i, pw_i, gate_w, alpha_raw)

    def _L0_attn_b_ref(x, W_in, b_in, W_out, b_out, rel_emb):
        import jax, jax.numpy as jnp
        import numpy as np
        MAX_POSITION = 1024
        EMBED_DIM = 256
        NUM_HEADS = 16
        HEAD_DIM = EMBED_DIM // NUM_HEADS
        B, S = (2, 512)
        b, s, e = x.shape
        h, d = (NUM_HEADS, HEAD_DIM)
        pos = jnp.arange(s)
        diff = jnp.clip(pos[None, :] - pos[:, None] + MAX_POSITION - 1, 0, MAX_POSITION - 1)
        emb = rel_emb[diff]
        bias = jnp.broadcast_to(emb.reshape(h, s, s)[None], (b, h, s, s))
        qkv = x @ W_in + b_in
        q, k, v = jnp.split(qkv, 3, axis=-1)
        split = lambda t: t.reshape(b, s, h, d).transpose(0, 2, 1, 3)
        q, k, v = (split(q), split(k), split(v))
        scores = jnp.einsum('bhqd,bhkd->bhqk', q, k) / jnp.sqrt(jnp.float32(d)).astype(x.dtype)
        attn = jax.nn.softmax(scores + bias, axis=-1)
        out = jnp.einsum('bhqk,bhkd->bhqd', attn, v)
        out = out.transpose(0, 2, 1, 3).reshape(b, s, e)
        return out @ W_out + b_out

    def _L0_ffn_ref(x, gate_w, gate_b, expert_w, expert_b):
        import jax, jax.numpy as jnp
        import numpy as np
        B, S, D, O, E, K = (4, 512, 256, 256, 8, 2)
        logits = jnp.einsum('bsd,ed->bse', x, gate_w) + gate_b
        if K < E:
            topv, topi = jax.lax.top_k(logits, K)
            keep = jax.nn.one_hot(topi, E, dtype=jnp.float32).sum(axis=-2)
            logits = jnp.where(keep > 0, logits, -jnp.inf)
        gate_score = jax.nn.softmax(logits, axis=-1)
        expert_out = jnp.einsum('bsd,edo->bseo', x, expert_w) + expert_b
        out = jnp.einsum('bseo,bse->bso', expert_out, gate_score)
        return out
    x = L0_attn_a_hidden_states
    x = x + _L0_attn_a_ref(_layernorm(x, axis=-1), L0_attn_a_q_w, L0_attn_a_k_w, L0_attn_a_v_w, L0_attn_a_o_w, L0_attn_a_dw_r, L0_attn_a_pw_r, L0_attn_a_dw_i, L0_attn_a_pw_i, L0_attn_a_gate_w, L0_attn_a_alpha_raw)
    x = x + _L0_ffn_ref(_layernorm(x, axis=-1), L0_ffn_gate_w, L0_ffn_gate_b, L0_ffn_expert_w, L0_ffn_expert_b)
    x = x + _L0_attn_b_ref(_layernorm(x, axis=-1), L0_attn_b_W_in, L0_attn_b_b_in, L0_attn_b_W_out, L0_attn_b_b_out, L0_attn_b_rel_emb)
    x = x + _L0_ffn_ref(_layernorm(x, axis=-1), L0_ffn_gate_w, L0_ffn_gate_b, L0_ffn_expert_w, L0_ffn_expert_b)
    return x

_drawn_inputs = setup_inputs


def setup_inputs(seed=0):
    import zlib

    import numpy as np

    out = dict(_drawn_inputs(seed))
    spreads = {'L0_attn_b_b_in': (0.0, 0.1), 'L0_attn_b_b_out': (0.0, 0.1)}
    factors = {'L0_attn_a_gate_w': 24.202, 'L0_attn_b_rel_emb': 36.033}
    for name, (base, spread) in spreads.items():
        noise = np.random.default_rng([zlib.crc32(name.encode()), seed]).standard_normal(out[name].shape)
        drawn = base * np.exp(spread * noise) if base else spread * noise
        out[name] = jnp.asarray(drawn.astype(out[name].dtype))
    for name, factor in factors.items():
        out[name] = (out[name] * factor).astype(out[name].dtype)
    return out
```

```python
from contextlib import ExitStack

import concourse.bass as bass
from concourse import mybir

F32 = mybir.dt.float32
F16 = mybir.dt.float16
BF16 = mybir.dt.bfloat16
I32 = mybir.dt.int32
U32 = mybir.dt.uint32
ALU = mybir.AluOpType
ACT = mybir.ActivationFunctionType
AX = mybir.AxisListType
RMAX = bass.bass_isa.ReduceOp.max

P = 128
EPS = 1e-5
LN_SCALE = 1024.0
W_TOP = 2.0 ** 14


def wait_alone(eng, sem, value, passed):
    eng.wait_ge(sem, value)
    eng.sem_inc(passed, 1)


def need(eng, s, value):
    if not (isinstance(value, int) and value <= 0):
        eng.wait_ge(s, value)


def need_alone(eng, sem, value, passed):
    if not (isinstance(value, int) and value <= 0):
        wait_alone(eng, sem, value, passed)


def spectral_layer(nc, C):
    with ExitStack() as outer:
        C.xlow = outer.enter_context(nc.sbuf_tensor("a_xlow", [P, C.D // P, C.B, 2, C.S // C.CH * C.LOW], F32))
        with ExitStack() as ctx:
            kd, nch = C.D // P, C.B * C.S // C.CH
            C.x_re = ctx.enter_context(nc.sbuf_tensor("a_x_re", [P, kd, nch, C.TAPS - 1 + C.NRE], F32))
            C.x_im = ctx.enter_context(nc.sbuf_tensor("a_x_im", [P, kd, nch, C.TAPS - 1 + C.NIM], F32))
            C.gT = ctx.enter_context(nc.sbuf_tensor("a_gT", [P, C.D // P, C.B * C.S // C.CH], F32))
            transform(nc, C)
            mix_high(nc, C)
        attend_low(nc, C)


def transform(nc, C):
    D, B, S, CH, LOW, TAPS, NRE, NIM, NT = C.D, C.B, C.S, C.CH, C.LOW, C.TAPS, C.NRE, C.NIM, C.NT
    KD = D // P
    TG = S // P
    NC2 = P // CH
    NCH = B * S // CH
    LC = 2 * NC2 * LOW
    xres, xlow, x_re, x_im = C.xres, C.xlow, C.x_re, C.x_im
    with ExitStack() as ctx:
        def sb(name, shape, dt=F32):
            return ctx.enter_context(nc.sbuf_tensor(f"t_{name}", shape, dt))

        def sem(name):
            return ctx.enter_context(nc.semaphore(f"t_{name}"))

        dft_ps = [ctx.enter_context(nc.psum_tensor(f"t_dft_ps{n}", [P, KD, 256], F32)) for n in range(4)]
        gate_ps = ctx.enter_context(nc.psum_tensor("t_gate_ps", [P, KD, NCH], F32))
        NF = LC + NC2 * (NRE + NIM)
        dft = sb("dft", [P, NF])
        gate_wT = sb("gate_wT", [P, KD, D])
        stats = sb("stats", [P, TG, 6])
        mv = sb("mv", [P, TG, 2])
        var_eps = sb("var_eps", [P, TG])
        rstd = sb("rstd", [P, TG])
        mhalf = sb("mhalf", [P, TG])
        xn = sb("xn", [P, 2, TG, D])
        eg = sb("eg", [P, KD, NCH])

        loaded = sem("loaded")
        const_ready = sem("const_ready")
        stats_ready = sem("stats_ready")
        mv_ready = sem("mv_ready")
        var_ready = sem("var_ready")
        rstd_ready = sem("rstd_ready")
        xn_ready = sem("xn_ready")
        added = sem("added")
        dft_done = sem("dft_done")
        act_took = sem("act_took")
        dve_took = sem("dve_took")
        gate_done = sem("gate_done")
        exp_ready = sem("exp_ready")
        gate_step = sem("gate_step")
        v_passed = sem("v_passed")
        p_passed = sem("p_passed")

        def all_batches(eng, group):
            group(0, 0, False)
            group(1, 1, False)
            with eng.Fori(1, B // 2 - 1) as i:
                group(i * 2, 0, False)
                group(i * 2 + 1, 1, False)
            group(B - 2, 0, False)
            group(B - 1, 1, True)

        def take(eng, b, j, took):
            at = LC + NC2 * NRE
            eng.wait_ge(dft_done, b * TG + j + 1)
            for out, lo, hi, nf in (
                    (xlow[:, :, bass.ds(b, 1), :, j * NC2 * LOW:(j + 1) * NC2 * LOW].rearrange("p k a r f -> p k (a r) f"),
                     0, LC, NC2 * LOW),
                    (x_re[:, :, bass.ds(b * (TG * NC2) + j * NC2, NC2), TAPS - 1:], LC, at, NRE),
                    (x_im[:, :, bass.ds(b * (TG * NC2) + j * NC2, NC2), TAPS - 1:], at, NF, NIM)):
                src = dft_ps[j][:, :, lo:hi].rearrange("p k (c f) -> p k c f", f=nf)
                if took is act_took:
                    eng.activation(out, src, ACT.Copy).then_inc(took, 1)
                else:
                    eng.tensor_copy(out, src).then_inc(took, 1)

        with nc.Block() as block:
            @block.sync
            def _(sp):
                sp.dma_start(dft[:, :], C.dft).then_inc(loaded, 16)
                sp.dma_start(gate_wT[:, :, :], C.a_gate_wT.rearrange("(k p) e -> p k e", p=P)).then_inc(loaded, 16)

            @block.gpsimd
            def _(pool):
                pool.memset(mhalf[:, :], -0.5).then_inc(const_ready, 1)
                pool.memset(x_re[:, :, :, 0:TAPS - 1], 0.0).then_inc(const_ready, 1)
                pool.memset(x_im[:, :, :, 0:TAPS - 1], 0.0).then_inc(const_ready, 1)
                pool.wait_ge(const_ready, 3)

                def rstd_of(b):
                    wait_alone(pool, mv_ready, b * TG + TG, p_passed)
                    pool.tensor_scalar(var_eps[:, :], mv[:, :, 1], EPS, None, ALU.add).then_inc(var_ready, 1)
                    pool.wait_ge(var_ready, b + 1)
                    pool.tensor_tensor(rstd[:, :], var_eps[:, :], mhalf[:, :], ALU.pow).then_inc(rstd_ready, 1)

                def group(b, par, last):
                    if not last:
                        rstd_of(b + 1)
                    pool.wait_ge(xn_ready, b * TG + TG)
                    rows = xres[:, bass.ds(b * TG, TG), :]
                    pool.tensor_tensor(rows, rows, xn[:, par, :, :], ALU.add).then_inc(added, 1)

                rstd_of(0)
                all_batches(pool, group)

            @block.scalar
            def _(act):
                def group(b, par, last):
                    for j in range(TG - 1):
                        take(act, b, j, act_took)

                all_batches(act, group)
                act.wait_ge(gate_done, 1)
                act.activation(eg[:, :, :], gate_ps[:, :, :], ACT.Exp, scale=-1.0 / CH).then_inc(exp_ready, 1)

            @block.vector
            def _(dve):
                def layernorm(b, par):
                    for j in range(TG):
                        dve.bn_stats(stats[:, j, :], xres[:, bass.ds(b * TG + j, 1), :].rearrange("p a d -> p (a d)")
                                     ).then_inc(stats_ready, 1)
                    wait_alone(dve, stats_ready, b * TG + TG, v_passed)
                    for j in range(TG):
                        dve.bn_aggr(mv[:, j, :], stats[:, j, :]).then_inc(mv_ready, 1)
                    need(dve, dft_done, b * TG - TG)
                    need(dve, added, b - 1)
                    dve.wait_ge(rstd_ready, b + 1)
                    for j in range(TG):
                        dve.tensor_scalar(xn[:, par, j, :], xres[:, bass.ds(b * TG + j, 1), :].rearrange("p a d -> p (a d)"),
                                          mv[:, j, 0:1], rstd[:, j:j + 1], ALU.subtract, ALU.mult).then_inc(xn_ready, 1)

                def group(b, par, last):
                    if not last:
                        layernorm(b + 1, 1 - par)
                    take(dve, b, TG - 1, dve_took)

                layernorm(0, 0)
                all_batches(dve, group)
                dve.wait_ge(exp_ready, 1)
                dve.tensor_scalar(eg[:, :, :], eg[:, :, :], 1.0, None, ALU.add).then_inc(gate_step, 1)
                dve.wait_ge(gate_step, 1)
                dve.reciprocal(C.gT[:, :, :], eg[:, :, :]).then_inc(gate_step, 1)

            @block.tensor
            def _(pe):
                pe.wait_ge(loaded, 32)

                def group(b, par, last):
                    for j in range(TG):
                        pe.wait_ge(xn_ready, b * TG + j + 1)
                        if j < TG - 1:
                            need(pe, act_took, b * (3 * (TG - 1)) + (j + 2 - TG) * 3)
                        else:
                            need(pe, dve_took, b * 3)
                        for k in range(KD):
                            ins = pe.matmul(dft_ps[j][:, k, 0:NF], xn[:, par, j, k * P:(k + 1) * P], dft[:, :],
                                            start=True, stop=True)
                        ins.then_inc(dft_done, 1)

                all_batches(pe, group)
                pe.wait_ge(act_took, B * 3 * (TG - 1))
                pe.wait_ge(dve_took, B * 3)
                for o in range(KD):
                    for k in range(KD):
                        ins = pe.matmul(gate_ps[:, o, :], gate_wT[:, k, o * P:(o + 1) * P],
                                        xlow[:, k, :, 0, :].rearrange("p b (c f) -> p b c f", f=LOW)[:, :, :, 0],
                                        start=(k == 0), stop=(k == KD - 1))
                ins.then_inc(gate_done, 1)


def mix_high(nc, C):
    D, B, S, CH, TAPS, NRE, NIM = C.D, C.B, C.S, C.CH, C.TAPS, C.NRE, C.NIM
    KD = D // P
    TG = S // P
    NC2 = P // CH
    NB = S // CH
    NCH = B * NB
    RE, IM = NB * NRE, NB * NIM
    TR, TI = NC2 * NRE, NC2 * NIM
    xres, x_re, x_im, gT, ident = C.xres, C.x_re, C.x_im, C.gT, C.ident
    with ExitStack() as ctx:
        def sb(name, shape, dt=F32):
            return ctx.enter_context(nc.sbuf_tensor(f"h_{name}", shape, dt))

        def sem(name):
            return ctx.enter_context(nc.semaphore(f"h_{name}"))

        mix_ps = [ctx.enter_context(nc.psum_tensor(f"h_mix_ps{o}", [P, 512], F32)) for o in range(KD)]
        turn_ps = [ctx.enter_context(nc.psum_tensor(f"h_turn_ps{n}", [P, 2, KD, P], F32)) for n in range(2)]
        out_ps = [ctx.enter_context(nc.psum_tensor(f"h_out_ps{n}", [P, 2, D], F32)) for n in range(2)]
        taps = sb("taps", [P, 2, KD, TAPS])
        pwT = sb("pwT", [P, 2, KD, D])
        idft = sb("idft", [P, P])
        filt = sb("filt", [P, KD, RE + IM])
        act_f = sb("act_f", [P, KD, RE + IM])
        hT = sb("hT", [P, KD, TG, P])
        h = sb("h", [P, TG, KD, P])

        loaded = sem("loaded")
        zeroed = sem("zeroed")
        filt_step = sem("filt_step")
        act_done = sem("act_done")
        mixed = sem("mixed")
        gated = sem("gated")
        turned = sem("turned")
        h_ready = sem("h_ready")
        inverted = sem("inverted")
        added = sem("added")

        PIECES = [(k, r) for k in range(KD) for r in range(2)]
        NP_ = len(PIECES)
        STEPS = TAPS * NP_

        def columns(r):
            return (0, RE) if r == 0 else (RE, RE + IM)

        def pipelined(eng, slot):
            for i in range(2):
                slot(i, i)
            with eng.Fori(2, B) as i:
                slot(i, None)
            for i in range(B, B + 2):
                slot(i, i)

        def exists(at, delay):
            return at is None or 0 <= at - delay < B

        with nc.Block() as block:
            @block.sync
            def _(sp):
                for r in range(2):
                    sp.dma_start(taps[:, r, :, :], C.dw[r].rearrange("(k p) o t -> p k (o t)", p=P)).then_inc(loaded, 16)
                    sp.dma_start(pwT[:, r, :, :], C.pwT[r].rearrange("(k p) e -> p k e", p=P)).then_inc(loaded, 16)
                sp.dma_start(idft[:, :], C.idft_high).then_inc(loaded, 16)

            @block.gpsimd
            def _(pool):
                pool.memset(hT[:, :, :, TR + TI:], 0.0).then_inc(zeroed, 1)

            @block.scalar
            def _(act):
                def slot(i, at):
                    if exists(at, 0):
                        for n, (k, r) in enumerate(PIECES):
                            lo, hi = columns(r)
                            act.wait_ge(filt_step, i * STEPS + (STEPS - NP_ + n + 1))
                            if n == 0:
                                need(act, mixed, i * KD)
                            act.activation(act_f[:, k, lo:hi], filt[:, k, lo:hi], ACT.Gelu).then_inc(act_done, 1)
                    if exists(at, 1):
                        for n in range(2):
                            act.wait_ge(turned, i * 2 + (n - 1))
                            if n == 0:
                                need(act, inverted, i * 2 - 2)
                            act.activation(h[:, 2 * n:2 * n + 2, :, :], turn_ps[n][:, :, :, :], ACT.Copy).then_inc(h_ready, 1)

                pipelined(act, slot)

            @block.vector
            def _(dve):
                dve.wait_ge(loaded, 16 * 5)

                def filter_batch(b):
                    for t in range(TAPS):
                        for n, (k, r) in enumerate(PIECES):
                            lo, hi = columns(r)
                            nf = (NRE, NIM)[r]
                            acc = filt[:, k, lo:hi].rearrange("p (c f) -> p c f", f=nf)
                            src = (x_re, x_im)[r][:, k, bass.ds(b * NB, NB), t:t + nf]
                            if t == 0:
                                need(dve, act_done, b * NP_ + (n + 1 - NP_))
                                dve.tensor_scalar(acc, src, taps[:, r, k, t:t + 1], None, ALU.mult).then_inc(filt_step, 1)
                            else:
                                dve.wait_ge(filt_step, b * STEPS + ((t - 1) * NP_ + n + 1))
                                dve.scalar_tensor_tensor(acc, src, taps[:, r, k, t:t + 1], acc, ALU.mult,
                                                         ALU.add).then_inc(filt_step, 1)

                def gate_batch(i):
                    for o in range(KD):
                        dve.wait_ge(mixed, i * KD + (o + 1 - KD))
                        if o == 0:
                            need(dve, turned, i * 2 - 2)
                        for r in range(2):
                            lo, hi = columns(r)
                            nf = (NRE, NIM)[r]
                            t0 = (0, TR)[r]
                            g = gT[:, o, bass.ds(i * NB - NB, NB)].rearrange("p (t c) -> p t c", c=NC2)
                            dve.tensor_tensor(hT[:, o, :, t0:t0 + NC2 * nf].rearrange("p t (c f) -> p t c f", f=nf),
                                              mix_ps[o][:, lo:hi].rearrange("p (t c f) -> p t c f", c=NC2, f=nf),
                                              g.unsqueeze(3).broadcast_to([P, TG, NC2, nf]), ALU.mult).then_inc(gated, 1)

                def slot(i, at):
                    if exists(at, 0):
                        filter_batch(i)
                    if exists(at, 1):
                        gate_batch(i)
                    if exists(at, 2):
                        for n in range(2):
                            dve.wait_ge(inverted, i * 2 + (n - 3))
                            rows = xres[:, bass.ds(i * TG + (2 * n - 2 * TG), 2), :]
                            dve.tensor_tensor(rows, rows, out_ps[n][:, :, :], ALU.add).then_inc(added, 1)

                pipelined(dve, slot)

            @block.tensor
            def _(pe):
                pe.wait_ge(loaded, 16 * 5)
                pe.wait_ge(zeroed, 1)

                def slot(i, at):
                    if exists(at, 0):
                        pe.wait_ge(act_done, i * NP_ + NP_)
                        for o in range(KD):
                            need(pe, gated, i * (2 * KD) + (2 * o + 2 - 2 * KD))
                            for r in range(2):
                                lo, hi = columns(r)
                                for k in range(KD):
                                    ins = pe.matmul(mix_ps[o][:, lo:hi], pwT[:, r, k, o * P:(o + 1) * P], act_f[:, k, lo:hi],
                                                    start=(k == 0), stop=(k == KD - 1))
                            ins.then_inc(mixed, 1)
                    if exists(at, 1):
                        pe.wait_ge(gated, i * (2 * KD))
                        for n in range(2):
                            need(pe, h_ready, i * 2 + (n - 3))
                            for t in range(2):
                                for o in range(KD):
                                    ins = pe.transpose(turn_ps[n][:, t, o, :], hT[:, o, 2 * n + t, :], ident[:, :])
                            ins.then_inc(turned, 1)
                        for n in range(2):
                            pe.wait_ge(h_ready, i * 2 + (n - 1))
                            need(pe, added, i * 2 + (n - 3))
                            for t in range(2):
                                ins = pe.matmul(out_ps[n][:, t, :], idft[:, :], h[:, 2 * n + t, :, :].rearrange("p o c -> p (o c)"),
                                                start=True, stop=True)
                            ins.then_inc(inverted, 1)

                pipelined(pe, slot)


def attend_low(nc, C):
    D, B, S, NT = C.D, C.B, C.S, C.NT
    KD = D // P
    HD, NKV = C.HD, C.NKV
    REP = 4
    NQ = REP * NKV * HD // P
    G = B // 2
    xres, ident = C.xres, C.ident
    with ExitStack() as ctx:
        def sb(name, shape, dt=F32):
            return ctx.enter_context(nc.sbuf_tensor(f"l_{name}", shape, dt))

        def sem(name):
            return ctx.enter_context(nc.semaphore(f"l_{name}"))

        ps = [ctx.enter_context(nc.psum_tensor(f"l_ps{n}", [P, 512], F32)) for n in range(8)]
        s_ps, t_ps, o_ps, proj_ps, out_ps = ps[0:2], ps[2:4], ps[4], ps[5], ps[6:8]

        q_wT = sb("q_wT", [P, KD, NQ * P])
        k_wT = sb("k_wT", [P, KD, NKV, 2, HD])
        v_wT = sb("v_wT", [P, KD, NKV, 2, HD])
        o_wT = sb("o_wT", [P, NQ, D])
        idft = sb("idft", [P, 2 * NT // B, P])
        mask = sb("mask", [P, P])
        neg_ident = sb("neg_ident", [P, P])
        alpha = sb("alpha", [P, 1])
        alpha_e = sb("alpha_e", [P, 1])
        alpha_d = sb("alpha_d", [P, 1])
        qT = sb("qT", [P, NQ, G, P])
        kT = sb("kT", [P, G, NKV, 2, P])
        v = sb("v", [P, G, NKV * 2 * HD])
        masked = sb("masked", [P, 2, REP, P])
        neg_max = sb("neg_max", [P, 2, REP])
        probs = sb("probs", [P, 2, REP, P])
        sums = sb("sums", [P, 2, REP])
        recip = sb("recip", [P, 2, REP])
        normed = sb("normed", [P, 2, REP, P])
        probsT = sb("probsT", [P, 2, REP, P])
        oT = sb("oT", [P, NQ, P])
        low = sb("low", [P, D])

        loaded = sem("loaded")
        const_ready = sem("const_ready")
        alpha_step = sem("alpha_step")
        alpha_exp = sem("alpha_exp")
        proj_done = sem("proj_done")
        act_took = sem("act_took")
        dve_took = sem("dve_took")
        scored = sem("scored")
        masked_done = sem("masked_done")
        exp_done = sem("exp_done")
        recip_done = sem("recip_done")
        normed_done = sem("normed_done")
        turned = sem("turned")
        pt_ready = sem("pt_ready")
        weighed = sem("weighed")
        o_ready = sem("o_ready")
        mixed = sem("mixed")
        low_ready = sem("low_ready")
        inverted = sem("inverted")
        added = sem("added")
        v_passed = sem("v_passed")

        def x_rows(k, g):
            return C.xlow[:, k, bass.ds(g * 2, 2), :, :].rearrange("p b r f -> p (b r f)")

        UNITS = ([("q", m, n) for n in range(2) for m in range(NQ)] + [("k", j, n) for n in range(2) for j in range(NKV)] +
                 [("v", 0, g) for g in range(G)])
        HG = G // 2

        def taken_count(parity, upto):
            return sum(2 if UNITS[n][0] == "k" else 1 for n in range(upto) if n % 2 == parity)

        def take_units(eng, parity, done):
            for n, (what, m, at) in enumerate(UNITS):
                if n % 2 != parity:
                    continue
                eng.wait_ge(proj_done, n + 1)
                src = ps[n % 8]
                if what == "q":
                    pairs = [(qT[:, m, HG * at:HG * (at + 1), :], src[:, :].rearrange("p (g c) -> p g c", c=P), -HD ** -0.5)]
                elif what == "k":
                    pairs = [(kT[HD * e:HD * (e + 1), HG * at:HG * (at + 1), m, e, :],
                              src[HD * e:HD * (e + 1), :].rearrange("p (g c) -> p g c", c=P), 1.0) for e in range(2)]
                else:
                    pairs = [(v[:, at, :], src[:, :], 1.0)]
                for out, in_, scale in pairs:
                    if parity == 0:
                        eng.activation(out, in_, ACT.Copy, scale=scale).then_inc(done, 1)
                    elif scale == 1.0:
                        eng.tensor_copy(out, in_).then_inc(done, 1)
                    else:
                        eng.tensor_scalar(out, in_, scale, None, ALU.mult).then_inc(done, 1)

        def all_groups(eng, group):
            for g in range(G + 2):
                group(g, g)

        def unit(g, at, j, delay):
            back = (delay - j + NKV - 1) // NKV if delay > j else 0
            if at is not None and not 0 <= at * NKV + j - delay < G * NKV:
                return None
            return g - back, j - delay + back * NKV

        with nc.Block() as block:
            @block.sync
            def _(sp):
                sp.dma_start(q_wT[:, :, :], C.q_wT.rearrange("(k p) e -> p k e", p=P)).then_inc(loaded, 16)
                for w, src in ((k_wT, C.k_wT), (v_wT, C.v_wT)):
                    for k in range(KD):
                        for e in range(2):
                            sp.dma_start(w[:, k, :, e, :], src[k * P:(k + 1) * P, :].rearrange("p (j d) -> p j d", d=HD)
                                         ).then_inc(loaded, 16)
                sp.dma_start(o_wT[:, :, :], C.o_wT.rearrange("(m p) e -> p m e", p=P)).then_inc(loaded, 16)
                sp.dma_start(idft[:, :, :], C.idft_low.rearrange("t p c -> p t c")).then_inc(loaded, 16)
                sp.dma_start(mask[:, :], C.mask).then_inc(loaded, 16)
                sp.dma_start(alpha[:, :], C.alpha_raw.unsqueeze(0).broadcast_to([P, 1])).then_inc(loaded, 16)

            LOADS = 16 * (5 + 4 * KD)

            @block.gpsimd
            def _(pool):
                pool.memset(kT[0:HD, :, :, 1, :], 0.0).then_inc(const_ready, 1)
                pool.memset(kT[HD:P, :, :, 0, :], 0.0).then_inc(const_ready, 1)
                pool.wait_ge(const_ready, 2)
                pool.tensor_scalar(neg_ident[:, :], ident[:, :], -1.0, None, ALU.mult).then_inc(const_ready, 1)

                def group(g, at):
                    for j in range(NKV):
                        u = unit(g, at, j, 1)
                        if u:
                            n = u[0] * NKV + u[1]
                            pool.wait_ge(recip_done, n + 1)
                            need(pool, turned, n - 1)
                            pool.tensor_tensor(normed[:, u[1] % 2, :, :], probs[:, u[1] % 2, :, :],
                                               recip[:, u[1] % 2, :].unsqueeze(2).broadcast_to([P, REP, P]),
                                               ALU.mult).then_inc(normed_done, 1)

                all_groups(pool, group)

            @block.scalar
            def _(act):
                act.wait_ge(loaded, LOADS)
                act.activation(alpha_e[:, :], alpha[:, :], ACT.Exp, scale=-1.0).then_inc(alpha_exp, 1)
                take_units(act, 0, act_took)

                def group(g, at):
                    for j in range(NKV):
                        u = unit(g, at, j, 0)
                        if u:
                            n = u[0] * NKV + u[1]
                            act.wait_ge(masked_done, n * REP + REP)
                            need(act, normed_done, n - 1)
                            for h in range(REP):
                                act.activation(probs[:, j % 2, h, :], masked[:, j % 2, h, :], ACT.Exp, scale=-1.0,
                                               bias=neg_max[:, j % 2, h:h + 1],
                                               accum_out=sums[:, j % 2, h:h + 1]).then_inc(exp_done, 1)
                        u = unit(g, at, j, 2)
                        if u:
                            n = u[0] * NKV + u[1]
                            act.wait_ge(turned, n + 1)
                            need(act, weighed, n - 1)
                            act.activation(probsT[:, u[1] % 2, :, :], t_ps[u[1] % 2][:, :].rearrange("p (h c) -> p h c", c=P),
                                           ACT.Copy).then_inc(pt_ready, 1)
                    if at is None or 0 <= at - 1 < G:
                        act.wait_ge(mixed, g)
                        need(act, inverted, (g - 1) * NKV)
                        act.activation(low[:, :], proj_ps[:, 0:D], ACT.Copy, scale=alpha[:, 0:1]).then_inc(low_ready, 1)

                act.wait_ge(alpha_step, 2)
                all_groups(act, group)

            @block.vector
            def _(dve):
                dve.wait_ge(alpha_exp, 1)
                dve.tensor_scalar(alpha_d[:, :], alpha_e[:, :], 1.0, None, ALU.add).then_inc(alpha_step, 1)
                dve.wait_ge(alpha_step, 1)
                dve.reciprocal(alpha[:, :], alpha_d[:, :]).then_inc(alpha_step, 1)
                take_units(dve, 1, dve_took)

                def group(g, at):
                    for j in range(NKV):
                        u = unit(g, at, j, 0)
                        if u:
                            n = u[0] * NKV + u[1]
                            need_alone(dve, exp_done, (n - 1) * REP, v_passed)
                            wait_alone(dve, scored, n + 1, v_passed)
                            for h in range(REP):
                                dve.tensor_tensor_reduce(out=masked[:, j % 2, h, :], in0=s_ps[j % 2][:, h * P:(h + 1) * P],
                                                         in1=mask[:, :], scale=1.0, scalar=3e38, op0=ALU.add, op1=ALU.min,
                                                         accum_out=neg_max[:, j % 2, h:h + 1]).then_inc(masked_done, 1)
                        u = unit(g, at, j, 1)
                        if u:
                            n = u[0] * NKV + u[1]
                            dve.wait_ge(exp_done, n * REP + REP)
                            need(dve, normed_done, n - 1)
                            dve.reciprocal(recip[:, u[1] % 2, :], sums[:, u[1] % 2, :]).then_inc(recip_done, 1)
                        u = unit(g, at, j, 3)
                        if u:
                            n = u[0] * NKV + u[1]
                            dve.wait_ge(weighed, n + 1)
                            if u[1] == 0:
                                need(dve, mixed, u[0])
                            for e in range(2):
                                dve.tensor_copy(oT[HD * e:HD * (e + 1), 2 * u[1]:2 * u[1] + 2, :],
                                                o_ps[HD * e:HD * (e + 1), :].rearrange("p (m e c) -> p m e c", e=2, c=P)[:, :, e, :]
                                                ).then_inc(o_ready, 1)
                        if at is None or 0 <= at - 2 < G:
                            n = (g - 2) * NKV + j
                            dve.wait_ge(inverted, n + 1)
                            rows = xres[:, bass.ds(n * 2, 2), :]
                            dve.tensor_tensor(rows, rows, out_ps[j % 2][:, :].rearrange("p (t d) -> p t d", t=2),
                                              ALU.add).then_inc(added, 1)

                all_groups(dve, group)

            @block.tensor
            def _(pe):
                pe.wait_ge(loaded, LOADS)
                pe.wait_ge(const_ready, 3)
                for n, (what, m, at) in enumerate(UNITS):
                    if n >= 8:
                        pe.wait_ge((act_took, dve_took)[n % 2], taken_count(n % 2, n - 7))
                    for k in range(KD):
                        if what == "v":
                            pe_l, pe_r = x_rows(k, at), v_wT[:, k, :, :, :].rearrange("p j e d -> p (j e d)")
                        else:
                            pe_l = (q_wT[:, k, m * P:(m + 1) * P] if what == "q" else
                                    k_wT[:, k, m, :, :].rearrange("p e d -> p (e d)"))
                            pe_r = C.xlow[:, k, at * G:(at + 1) * G, :, :].rearrange("p b r f -> p (b r f)")
                        ins = pe.matmul(ps[n % 8][:, :], pe_l, pe_r, start=(k == 0), stop=(k == KD - 1))
                    ins.then_inc(proj_done, 1)
                pe.wait_ge(act_took, taken_count(0, len(UNITS)))
                pe.wait_ge(dve_took, taken_count(1, len(UNITS)))

                def group(g, at):
                    for j in range(NKV):
                        u = unit(g, at, j, 0)
                        if u:
                            n = u[0] * NKV + u[1]
                            need(pe, masked_done, (n - 1) * REP)
                            for m in range(2):
                                ins = pe.matmul(s_ps[j % 2][:, m * 2 * P:(m + 1) * 2 * P],
                                                qT[:, 2 * j + m, bass.ds(g, 1), :].rearrange("p a c -> p (a c)"),
                                                kT[:, bass.ds(g, 1), j, :, :].rearrange("p a e c -> p (a e c)"), start=True, stop=True)
                            ins.then_inc(scored, 1)
                        u = unit(g, at, j, 2)
                        if u:
                            n = u[0] * NKV + u[1]
                            pe.wait_ge(normed_done, n + 1)
                            need(pe, pt_ready, n - 1)
                            for h in range(REP):
                                ins = pe.transpose(t_ps[u[1] % 2][:, h * P:(h + 1) * P], normed[:, u[1] % 2, h, :], ident[:, :])
                            ins.then_inc(turned, 1)
                        u = unit(g, at, j, 3)
                        if u:
                            n = u[0] * NKV + u[1]
                            pe.wait_ge(pt_ready, n + 1)
                            need(pe, o_ready, n * 2)
                            pe.matmul(o_ps[:, :], v[:, bass.ds(u[0], 1), u[1] * 2 * HD:(u[1] + 1) * 2 * HD]
                                      .rearrange("p a d -> p (a d)"),
                                      probsT[:, u[1] % 2, :, :].rearrange("p h c -> p (h c)"), start=True,
                                      stop=True).then_inc(weighed, 1)
                        if at is None or 0 <= at - 2 < G:
                            n = (g - 2) * NKV + j
                            pe.wait_ge(low_ready, g - 1)
                            need(pe, added, n - 1)
                            for t in range(2):
                                ins = pe.matmul(out_ps[j % 2][:, t * D:(t + 1) * D], idft[:, 2 * j + t, :], low[:, :],
                                                start=True, stop=True)
                            ins.then_inc(inverted, 1)
                    if at is None or 0 <= at - 1 < G:
                        pe.wait_ge(o_ready, g * (2 * NKV))
                        need(pe, low_ready, g - 1)
                        for k in range(KD):
                            for m in range(NQ):
                                ins = pe.matmul(proj_ps[:, k * P:(k + 1) * P], oT[:, m, :], o_wT[:, m, k * P:(k + 1) * P],
                                                start=(m == 0), stop=False)
                            ins = pe.matmul(proj_ps[:, k * P:(k + 1) * P], x_rows(k, g - 1), neg_ident[:, :],
                                            start=False, stop=True)
                        ins.then_inc(mixed, 1)

                all_groups(pe, group)


def position_attention(nc, C):
    D, S, B, H = C.D, C.S, C.B, C.H
    HD = D // H
    KD = D // P
    QT = S // P
    HG = 4
    A = S // H
    UNIT = 8
    STEPS = H * QT
    UNITS = STEPS // UNIT
    TAIL = S + A
    xres, ident = C.xres, C.ident
    Q_PARTS = (0, 0, 1, 0, 2, 1)
    K_PARTS = (0, 1, 0, 2, 0, 1)
    NC_ = len(Q_PARTS)

    with ExitStack() as ctx:
        def sb(name, shape, dt=F32):
            return ctx.enter_context(nc.sbuf_tensor(f"b_{name}", shape, dt))

        def sem(name):
            return ctx.enter_context(nc.semaphore(f"b_{name}"))

        s_ps = [ctx.enter_context(nc.psum_tensor(f"b_s_ps{n}", [P, S], F32)) for n in range(2)]
        t_ps = [ctx.enter_context(nc.psum_tensor(f"b_t_ps{n}", [P, QT, P], F32)) for n in range(4)]
        o_ps = ctx.enter_context(nc.psum_tensor("b_o_ps", [P, 2, 2 * P], F32))
        misc = ctx.enter_context(nc.psum_tensor("b_misc", [P, 512], F32))

        ext_dram = nc.dram_tensor("b_ext", [TAIL + P - 1, H], F32, kind="Internal").ap()
        parts_dram = [nc.dram_tensor(f"b_{side}_parts", [2, P, 3, S], BF16, kind="Internal").ap() for side in "qk"]

        bias_tab = sb("bias_tab", [P, TAIL * H])
        stacks = [sb(f"{side}_stacks", [P, 2, HG, S], BF16) for side in "qk"]
        probsT = sb("probsT", [P, 2, HG, QT, 2 * P])
        w_in = sb("w_in", [P, KD, 3 * D])
        w_out = sb("w_out", [P, KD, D])
        b_cols = sb("b_cols", [P, 2, KD])
        b_v = sb("b_v", [P, D])
        b_o = sb("b_o", [P, D])
        stats = sb("stats", [P, 4, 6])
        mv = sb("mv", [P, 4, 2])
        var_eps = sb("var_eps", [P, 4])
        rstd = sb("rstd", [P, 4])
        mhalf = sb("mhalf", [P, 4])
        zero = sb("zero", [P, 1])
        xn = sb("xn", [P, QT, D])
        xnT = sb("xnT", [P, KD, S])
        v_sb = sb("v_sb", [P, QT, D + HD])
        probs = sb("probs", [P, 8, S])
        neg_max = sb("neg_max", [P, 8])
        sums = sb("sums", [P, 4, 2, HG])
        recip = sb("recip", [P, 2, 2, HG])
        proj = sb("proj", [P, 2, S])
        rest = sb("rest", [P, S])
        parts = sb("parts", [P, 2, 3, S], BF16)
        o_sb = sb("o_sb", [P, 2, 2 * P])
        o_tok = sb("o_tok", [P, QT, D])
        oT = sb("oT", [P, KD, S])

        loaded = sem("loaded")
        ext_written = sem("ext_written")
        tab_loaded = sem("tab_loaded")
        tab_ready = sem("tab_ready")
        const_ready = sem("const_ready")
        qb_ready = sem("qb_ready")
        stats_ready = sem("stats_ready")
        mv_ready = sem("mv_ready")
        var_ready = sem("var_ready")
        rstd_ready = sem("rstd_ready")
        xn_ready = sem("xn_ready")
        split_step = sem("split_step")
        written = [sem(f"{side}_written") for side in "qk"]
        stack_in = [sem(f"stack_in{n}") for n in range(2)]
        s_done = sem("s_done")
        biased_done = sem("biased_done")
        exp_done = sem("exp_done")
        turned = sem("turned")
        pt_even = sem("pt_even")
        pt_odd = sem("pt_odd")
        pv_done = sem("pv_done")
        o_taken = sem("o_taken")
        o_turned = sem("o_turned")
        o_scaled = sem("o_scaled")
        recip_done = sem("recip_done")
        misc_done = sem("misc_done")
        misc_free = sem("misc_free")
        preadded = sem("preadded")
        v_passed = sem("v_passed")
        p_passed = sem("p_passed")
        LEAD = 1
        LAG = 3
        READ = 16 * 2 * NC_

        USES = [(10, "v0"), (12, "v1"), (17, "oT0"), (18, "oT1"), (20, "out0"), (26, "out1"), (27, "xT0"), (28, "xT1"),
                (34, "qk0"), (36, "qk1"), (42, "qk2"), (50, "qk3")]
        OF_LAST_BATCH = ("oT0", "oT1", "out0", "out1")
        OF_NEXT_BATCH = ("xT0", "xT1", "qk0", "qk1", "qk2", "qk3")
        WEIGH, TAKE, TURN = 13, 15, 19
        names = {
            "start": list(OF_NEXT_BATCH),
            "first": [u for _, u in USES if u not in OF_LAST_BATCH],
            "mid": [u for _, u in USES],
            "last": [u for _, u in USES if u not in OF_NEXT_BATCH],
            "end": list(OF_LAST_BATCH),
        }

        def uses_before(b, kind, use):
            ahead, behind = len(OF_NEXT_BATCH), len(OF_LAST_BATCH)
            base = {"start": 0, "first": ahead, "mid": b * len(USES) + (ahead - behind),
                    "last": b * len(USES) + (ahead - behind), "end": b * len(USES) - behind}[kind]
            return base + names[kind].index(use)

        def all_batches(eng, slot):
            for t in range(STEPS):
                slot(0, "first", t)
            with eng.Fori(1, B - 1) as b:
                for t in range(STEPS):
                    slot(b, "mid", t)
            for t in range(STEPS):
                slot(B - 1, "last", t)
            for t in range(32):
                slot(B, "end", t)

        def in_step(kind, t, use, lead=0):
            return use in names[kind] and (t + lead, use) in USES

        def of_unit(kind, t, delay):
            return (t - delay) % UNIT == 0 and not (kind == "first" and t < delay) and not (kind == "end" and t >= delay)

        def evacuate(eng, b, t, ready):
            u, h, ql = t % STEPS // UNIT, t % UNIT // 2, t % 2
            if t % UNIT < 2:
                need(eng, pv_done, b * UNITS + t // UNIT - 1)
            eng.wait_ge(turned, b * STEPS + t + 1)
            dst = probsT[:, u % 2, h, :, ql * P:(ql + 1) * P]
            if ql == 0:
                eng.tensor_copy(dst, t_ps[t % 4][:, :, :]).then_inc(ready, 1)
            else:
                eng.activation(dst, t_ps[t % 4][:, :, :], ACT.Copy).then_inc(ready, 1)

        with nc.Block() as block:
            @block.sync
            def _(sp):
                sp.dma_start(ext_dram[0:S, :], C.rel_emb[S:2 * S, :]).then_inc(ext_written, 16)
                sp.dma_start(ext_dram[S:TAIL + P - 1, :],
                             C.rel_emb[2 * S - 1:2 * S, :].broadcast_to([TAIL + P - 1 - S, H])).then_inc(ext_written, 16)
                sp.dma_start(w_in[:, :, :], C.w_in.rearrange("(k p) e -> p k e", p=P)).then_inc(loaded, 16)
                sp.dma_start(w_out[:, :, :], C.w_out.rearrange("(k p) e -> p k e", p=P)).then_inc(loaded, 16)
                sp.dma_start(b_cols[:, :, :], C.b_in[0:2 * D].rearrange("(s k p) -> p s k", s=2, p=P),
                             allow_slow_non_contiguous=True).then_inc(loaded, 16)
                sp.dma_start(b_v[:, :], C.b_in[2 * D:3 * D].unsqueeze(0).broadcast_to([P, D])).then_inc(loaded, 16)
                sp.dma_start(b_o[:, :], C.b_out.unsqueeze(0).broadcast_to([P, D])).then_inc(loaded, 16)
                sp.wait_ge(ext_written, 32)
                sp.dma_start(bias_tab[:, :], bass.AP(tensor=ext_dram.tensor, offset=0,
                                                     ap=[[H, P], [1, TAIL * H]])).then_inc(tab_loaded, 16)

                def write(n, m, side):
                    sp.wait_ge(split_step, 8 * n + 4 * side + 4)
                    sp.dma_start(parts_dram[side][m], parts[:, side, :, :]).then_inc(written[side], 16)

                def read(g, pair):
                    m, slot = g // 2, g % 2
                    for side in range(2):
                        sp.wait_ge(written[side], 16 * pair + 16)
                        for c, part in enumerate((Q_PARTS, K_PARTS)[side]):
                            src = parts_dram[side][m, HG * HD * slot:HG * HD * (slot + 1), part, :]
                            sp.dma_start(stacks[side][HD * c:HD * (c + 1), slot, :, :],
                                         src.rearrange("(h d) q -> d h q", d=HD)).then_inc(stack_in[slot], 16)

                def batch(b, last):
                    sp.wait_ge(s_done, 16 * (b * 4 + 1))
                    read(2, b * 2 + 1)
                    sp.wait_ge(s_done, 16 * (b * 4 + 2))
                    read(3, b * 2 + 1)
                    if not last:
                        for slot in range(2):
                            sp.wait_ge(stack_in[slot], READ * (b * 2 + 1))
                        write(b * 2 + 2, 0, 0)
                        write(b * 2 + 2, 0, 1)
                        sp.wait_ge(s_done, 16 * (b * 4 + 3))
                        read(0, b * 2 + 2)
                        for slot in range(2):
                            sp.wait_ge(stack_in[slot], READ * (b * 2 + 2))
                        write(b * 2 + 3, 1, 0)
                        write(b * 2 + 3, 1, 1)
                        sp.wait_ge(s_done, 16 * (b * 4 + 4))
                        read(1, b * 2 + 2)

                for n in range(2):
                    write(n, n, 0)
                    write(n, n, 1)
                sp.wait_ge(const_ready, 1)
                read(0, 0)
                read(1, 0)
                with sp.Fori(0, B - 1) as b:
                    batch(b, False)
                batch(B - 1, True)
                for side in range(2):
                    sp.wait_ge(written[side], 16 * 2 * B)

            @block.gpsimd
            def _(pool):
                for side in range(2):
                    pool.memset(stacks[side][:, :, :, :].rearrange("p a h q -> p (a h q)"), 0.0).then_inc(tab_ready, 1)
                pool.wait_ge(tab_ready, 2)
                pool.memset(v_sb[:, :, D:], 0.0).then_inc(const_ready, 1)
                pool.memset(mhalf[:, :], -0.5).then_inc(const_ready, 1)
                pool.memset(zero[:, :], 0.0).then_inc(const_ready, 1)
                pool.wait_ge(const_ready, 3)
                pool.wait_ge(loaded, 16 * 5)
                pool.tensor_scalar(b_cols[:, 0, :], b_cols[:, 0, :], -HD ** -0.5, None, ALU.mult).then_inc(qb_ready, 1)

                def rstd_of(b):
                    wait_alone(pool, mv_ready, b * 4 + 4, p_passed)
                    pool.tensor_scalar(var_eps[:, :], mv[:, :, 1], EPS, None, ALU.add).then_inc(var_ready, 1)
                    pool.wait_ge(var_ready, b + 1)
                    pool.tensor_tensor(rstd[:, :], var_eps[:, :], mhalf[:, :], ALU.pow).then_inc(rstd_ready, 1)

                def split(b, kind, i):
                    nb = b if kind == "start" else b + 1
                    n, side = nb * 4 + i, i % 2
                    pool.wait_ge(misc_free, uses_before(b, kind, f"qk{i}") + 1)
                    need(pool, written[side], 16 * (nb * 2 + i // 2))
                    src, at = proj[:, side, :], n * 4
                    pool.tensor_tensor(parts[:, side, 0, :], src, zero[:, 0:1].broadcast_to([P, S]),
                                       ALU.add).then_inc(split_step, 1)
                    pool.wait_ge(split_step, at + 1)
                    pool.tensor_tensor(rest[:, :], src, parts[:, side, 0, :], ALU.subtract).then_inc(split_step, 1)
                    pool.wait_ge(split_step, at + 2)
                    pool.tensor_tensor(parts[:, side, 1, :], rest[:, :], zero[:, 0:1].broadcast_to([P, S]),
                                       ALU.add).then_inc(split_step, 1)
                    pool.wait_ge(split_step, at + 3)
                    pool.tensor_tensor(parts[:, side, 2, :], rest[:, :], parts[:, side, 1, :],
                                       ALU.subtract).then_inc(split_step, 1)

                def batch(b, kind):
                    pool.wait_ge(xn_ready, b * 4 + 4)
                    pool.tensor_tensor(xres[:, bass.ds(b * QT, QT), :], xres[:, bass.ds(b * QT, QT), :],
                                       b_o[:, :].unsqueeze(1).broadcast_to([P, QT, D]), ALU.add).then_inc(preadded, 1)
                    if kind != "last":
                        rstd_of(b + 1)
                        for i in range(4):
                            split(b, kind, i)

                rstd_of(0)
                for i in range(4):
                    split(0, "start", i)
                batch(0, "first")
                with pool.Fori(1, B - 1) as b:
                    batch(b, "mid")
                batch(B - 1, "last")

            @block.scalar
            def _(act):
                def take_xT(b, kind, k):
                    act.wait_ge(misc_done, uses_before(b, kind, f"xT{k}") + 1)
                    act.activation(xnT[:, k, :], misc[:, :], ACT.Copy).then_inc(misc_free, 1)

                def take_qk(b, kind, i):
                    nb = b if kind == "start" else b + 1
                    side, m = i % 2, i // 2
                    act.wait_ge(misc_done, uses_before(b, kind, f"qk{i}") + 1)
                    need(act, split_step, 4 * (nb * 4 + i - 1))
                    if side == 0:
                        act.activation(proj[:, 0, :].rearrange("p (b a) -> p a b", a=A)[:, ::-1, :],
                                       misc[:, :].rearrange("p (a b) -> p a b", a=A), ACT.Identity,
                                       bias=b_cols[:, 0, m:m + 1], scale=-HD ** -0.5).then_inc(misc_free, 1)
                    else:
                        act.activation(proj[:, 1, :], misc[:, :], ACT.Identity,
                                       bias=b_cols[:, 1, m:m + 1]).then_inc(misc_free, 1)

                def slot(b, kind, t):
                    if (t - LAG) % 2 == 0 and not (kind == "first" and t < LAG + 2) and not (kind == "end" and t > LAG):
                        evacuate(act, b, t - (LAG + 1), pt_odd)
                    if kind != "end":
                        u, T = t // UNIT, b * STEPS + t
                        h, ql = t % UNIT // 2, t % 2
                        act.wait_ge(biased_done, T + 1)
                        if t % UNIT == 0:
                            need(act, recip_done, b * UNITS + u - 3)
                        act.activation(probs[:, t % 8, :], probs[:, t % 8, :], ACT.Exp, bias=neg_max[:, t % 8:t % 8 + 1],
                                       scale=-1.0, accum_out=sums[:, u % 4, ql, h:h + 1]).then_inc(exp_done, 1)
                    if of_unit(kind, t, TAKE):
                        u = (t - TAKE) % STEPS // UNIT
                        n = b * UNITS + (t - TAKE) // UNIT
                        act.wait_ge(pv_done, n + 1)
                        need(act, recip_done, n - 1)
                        act.activation(o_sb[:, u % 2, :], o_ps[:, u % 2, :], ACT.Copy).then_inc(o_taken, 1)
                    for k in range(2):
                        if in_step(kind, t, f"xT{k}", LEAD):
                            take_xT(b, kind, k)
                        if in_step(kind, t, f"oT{k}", LEAD):
                            act.wait_ge(misc_done, uses_before(b, kind, f"oT{k}") + 1)
                            act.activation(oT[:, k, :].rearrange("p (a b) -> p b a", a=A)[:, :, ::-1],
                                           misc[:, :].rearrange("p (b a) -> p b a", a=A), ACT.Copy).then_inc(misc_free, 1)
                    for i in range(4):
                        if in_step(kind, t, f"qk{i}", LEAD):
                            take_qk(b, kind, i)

                act.wait_ge(qb_ready, 1)
                take_xT(0, "start", 0)
                take_xT(0, "start", 1)
                for i in range(4):
                    take_qk(0, "start", i)
                all_batches(act, slot)

            @block.vector
            def _(dve):
                def stats_of(b):
                    for j in range(QT):
                        dve.bn_stats(stats[:, j, :], xres[:, bass.ds(b * QT + j, 1), :].rearrange("p a d -> p (a d)")
                                     ).then_inc(stats_ready, 1)
                    wait_alone(dve, stats_ready, b * QT + QT, v_passed)
                    for j in range(QT):
                        dve.bn_aggr(mv[:, j, :], stats[:, j, :]).then_inc(mv_ready, 1)

                def norm(b, j):
                    if j == 0:
                        dve.wait_ge(rstd_ready, b + 1)
                    dve.tensor_scalar(xn[:, j, :], xres[:, bass.ds(b * QT + j, 1), :].rearrange("p a d -> p (a d)"),
                                      mv[:, j, 0:1], rstd[:, j:j + 1], ALU.subtract, ALU.mult).then_inc(xn_ready, 1)

                def slot(b, kind, t):
                    T = b * STEPS + t
                    if (t - LAG) % 2 and not (kind == "first" and t < LAG + 1) and not (kind == "end" and t > LAG):
                        evacuate(dve, b, t - (LAG + 1), pt_even)
                    if kind != "end":
                        h, qt = t // 16 * HG + t % UNIT // 2, t // UNIT % 2 * 2 + t % 2
                        window = min(P // A * qt - h, 1) + H - 1
                        need_alone(dve, turned, T - 7, v_passed)
                        wait_alone(dve, s_done, T + 1, v_passed)
                        dve.tensor_tensor_reduce(out=probs[:, t % 8, :], in0=s_ps[t % 2][:, :],
                                                 in1=bias_tab[:, window * S:(window + 1) * S], scale=1.0, scalar=3e38,
                                                 op0=ALU.add, op1=ALU.min,
                                                 accum_out=neg_max[:, t % 8:t % 8 + 1]).then_inc(biased_done, 1)
                    if of_unit(kind, t, TURN):
                        u = (t - TURN) % STEPS // UNIT
                        n = b * UNITS + (t - TURN) // UNIT
                        g, qp = u // 2, u % 2
                        dve.wait_ge(o_turned, n + 1)
                        dve.reciprocal(recip[:, u % 2, :, :], sums[:, u % 4, :, :]).then_inc(recip_done, 1)
                        if u == 0 and kind in ("mid", "last"):
                            dve.wait_ge(misc_done, uses_before(b, kind, "oT1") + 1)
                        dve.wait_ge(recip_done, n + 1)
                        dve.tensor_tensor(
                            o_tok[:, 2 * qp:2 * qp + 2, g * HG * HD:(g + 1) * HG * HD].rearrange("p q (h d) -> p q h d", h=HG),
                            o_ps[:, u % 2, :].rearrange("p (q h d) -> p q h d", q=2, h=HG)[:, :, :, 0:HD],
                            recip[:, u % 2, :, :].unsqueeze(3).broadcast_to([P, 2, HG, HD]),
                            ALU.mult).then_inc(o_scaled, 1)
                    for j in range(2):
                        if in_step(kind, t, f"v{j}", LEAD):
                            dve.wait_ge(misc_done, uses_before(b, kind, f"v{j}") + 1)
                            dve.tensor_tensor(v_sb[:, 2 * j:2 * j + 2, 0:D], misc[:, :].rearrange("p (t d) -> p t d", t=2),
                                              b_v[:, :].unsqueeze(1).broadcast_to([P, 2, D]), ALU.add).then_inc(misc_free, 1)
                        if in_step(kind, t, f"out{j}", LEAD):
                            rows = xres[:, bass.ds((b - 1) * QT + 2 * j, 2), :]
                            if j == 0:
                                dve.wait_ge(preadded, b)
                            dve.wait_ge(misc_done, uses_before(b, kind, f"out{j}") + 1)
                            dve.tensor_tensor(rows, rows, misc[:, :].rearrange("p (t d) -> p t d", t=2),
                                              ALU.add).then_inc(misc_free, 1)
                    if kind in ("first", "mid"):
                        if t == 14:
                            stats_of(b + 1)
                        if 18 <= t < 18 + QT:
                            norm(b + 1, t - 18)

                stats_of(0)
                for j in range(QT):
                    norm(0, j)
                dve.wait_ge(tab_loaded, 16)
                dve.tensor_scalar(bias_tab[:, :], bias_tab[:, :], -1.0, None, ALU.mult).then_inc(tab_ready, 1)
                dve.wait_ge(tab_ready, 3)
                dve.wait_ge(loaded, 16 * 5)
                all_batches(dve, slot)

            @block.tensor
            def _(pe):
                def bank(b, kind, use):
                    need(pe, misc_free, uses_before(b, kind, use))

                def turn_x(b, kind, k):
                    nb = b if kind == "start" else b + 1
                    pe.wait_ge(xn_ready, nb * QT + QT)
                    bank(b, kind, f"xT{k}")
                    for j in range(QT):
                        ins = pe.transpose(misc[:, j * P:(j + 1) * P], xn[:, j, k * P:(k + 1) * P], ident[:, :])
                    ins.then_inc(misc_done, 1)

                def project_qk(b, kind, i, k):
                    if k == 0:
                        bank(b, kind, f"qk{i}")
                    at = (i % 2) * D + (i // 2) * P
                    ins = pe.matmul(misc[:, :], w_in[:, k, at:at + P], xnT[:, k, :], start=(k == 0), stop=(k == KD - 1))
                    if k == KD - 1:
                        ins.then_inc(misc_done, 1)

                def project_rows(b, kind, use, j, i, rowsT, w):
                    if i == 0:
                        bank(b, kind, use)
                    for k in range(KD):
                        ins = pe.matmul(misc[:, i * D:(i + 1) * D], rowsT[:, k, (2 * j + i) * P:(2 * j + i + 1) * P],
                                        w[:, k, :], start=(k == 0), stop=(k == KD - 1))
                    if i == 1:
                        ins.then_inc(misc_done, 1)

                def weigh(b, kind, u, n, kt):
                    g = u // 2
                    if kt == 0:
                        pe.wait_ge(pt_even, 4 * n + 4)
                        pe.wait_ge(pt_odd, 4 * n + 4)
                        need(pe, o_scaled, n)
                    if u == 0 and kt % 2 == 0:
                        pe.wait_ge(misc_free, uses_before(b, kind, f"v{kt // 2}") + 1)
                    for h in range(HG):
                        head = g * HG + h
                        ins = pe.matmul(o_ps[32 * h:32 * (h + 1), u % 2, :], v_sb[:, kt, head * HD:head * HD + 32],
                                        probsT[:, u % 2, h, kt, :], start=(kt == 0), stop=(kt == QT - 1),
                                        tile_position=(0, 32 * h))
                    if kt == QT - 1:
                        ins.then_inc(pv_done, 1)

                def slot(b, kind, t):
                    T = b * STEPS + t
                    if kind != "end":
                        g = t // 16
                        h, qt = t % UNIT // 2, t // UNIT % 2 * 2 + t % 2
                        if t % 16 == 0:
                            pe.wait_ge(stack_in[g % 2], READ * (b * 2 + g // 2 + 1))
                        need(pe, biased_done, T - 1)
                        pe.matmul(s_ps[t % 2][:, :], stacks[0][:, g % 2, h, qt * P:(qt + 1) * P], stacks[1][:, g % 2, h, :],
                                  start=True, stop=True).then_inc(s_done, 1)
                    td = (t - LAG) % STEPS
                    if not (kind == "first" and t < LAG) and not (kind == "end" and t > LAG - 1):
                        pe.wait_ge(exp_done, T - (LAG - 1))
                        need(pe, (pt_even, pt_odd)[td % 2], b * (STEPS // 2) + (t - LAG - td % 2) // 2 - 1)
                        for kt in range(QT):
                            ins = pe.transpose(t_ps[td % 4][:, kt, :], probs[:, td % 8, kt * P:(kt + 1) * P], ident[:, :])
                        ins.then_inc(turned, 1)
                    for kt in range(QT):
                        if of_unit(kind, t, WEIGH + kt):
                            weigh(b, kind, (t - WEIGH - kt) % STEPS // UNIT, b * UNITS + (t - WEIGH - kt) // UNIT, kt)
                    if of_unit(kind, t, TURN):
                        u = (t - TURN) % STEPS // UNIT
                        pe.wait_ge(o_taken, b * UNITS + (t - TURN) // UNIT + 1)
                        for i in range(2):
                            ins = pe.transpose(o_ps[:, u % 2, i * P:(i + 1) * P], o_sb[:, u % 2, i * P:(i + 1) * P], ident[:, :])
                        ins.then_inc(o_turned, 1)
                    for j in range(2):
                        for i in range(2):
                            if in_step(kind, t, f"v{j}", 1 - i):
                                project_rows(b, kind, f"v{j}", j, i, xnT, w_in[:, :, 2 * D:3 * D])
                            if in_step(kind, t, f"out{j}", 1 - i):
                                project_rows(b, kind, f"out{j}", j, i, oT, w_out)
                        if in_step(kind, t, f"xT{j}"):
                            turn_x(b, kind, j)
                        if in_step(kind, t, f"oT{j}"):
                            bank(b, kind, f"oT{j}")
                            pe.wait_ge(o_scaled, b * UNITS)
                            for qt in range(QT):
                                ins = pe.transpose(misc[:, qt * P:(qt + 1) * P], o_tok[:, qt, j * P:(j + 1) * P], ident[:, :])
                            ins.then_inc(misc_done, 1)
                    for i in range(4):
                        for k in range(KD):
                            if in_step(kind, t, f"qk{i}", 1 - k):
                                project_qk(b, kind, i, k)

                pe.wait_ge(loaded, 16 * 5)
                pe.wait_ge(const_ready, 3)
                turn_x(0, "start", 0)
                turn_x(0, "start", 1)
                for i in range(4):
                    for k in range(KD):
                        project_qk(0, "start", i, k)
                all_batches(pe, slot)


def token_ffn(nc, C, which, out_dram):
    NT, D, E, TG = C.NT, C.D, C.E, C.TG
    KD = D // P
    NG = NT // TG
    xres, ident = C.xres, C.ident

    with ExitStack() as ctx:
        def sb(name, shape, dt=F32):
            return ctx.enter_context(nc.sbuf_tensor(f"{name}{which}", shape, dt))

        def sem(name):
            return ctx.enter_context(nc.semaphore(f"{name}{which}"))

        main = [ctx.enter_context(nc.psum_tensor(f"experts{n}_{which}", [P, 512], F32)) for n in range(4)]
        xT_ps = [ctx.enter_context(nc.psum_tensor(f"xT_ps{n}_{which}", [P, 512], F32)) for n in range(2)]
        small_ps = ctx.enter_context(nc.psum_tensor(f"small_ps_{which}", [P, 512], F32))
        bias_ps = ctx.enter_context(nc.psum_tensor(f"bias_ps_{which}", [P, 512], F32))
        logit_ps = small_ps[:, 0:TG * E].rearrange("p (t e) -> p t e", t=TG)
        gT_ps = small_ps[:, 128:256]

        w32 = sb("w32", [P, KD, E, D])
        w_hi = sb("w_hi", [P, KD, E * D], F16)
        w_lo = sb("w_lo", [P, KD, E * D], F16)
        gw32 = sb("gw32", [P, KD, E])
        gw_hi = sb("gw_hi", [P, KD, E], F16)
        gw_lo = sb("gw_lo", [P, KD, E], F16)
        gate_b = sb("gate_b", [P, TG, E])
        eb_rows = sb("eb_rows", [P, TG, D])
        wmax = sb("wmax", [P, 2])
        wmax_all = sb("wmax_all", [P, 2])
        scale = sb("scale", [P, 2])
        unscale = sb("unscale", [P, 2])
        wprod = sb("wprod", [P, D * E])
        iota8 = sb("iota8", [P, TG, E])
        stats = sb("stats", [P, TG, 6])
        mv = sb("mv", [P, TG, 2])
        var_eps = sb("var_eps", [P, TG])
        rstd = sb("rstd", [P, TG])
        mhalf = sb("mhalf", [P, TG])
        xn = sb("xn", [P, TG, D])
        xT_hi = sb("xT_hi", [P, 2, TG, KD, P], F16)
        xT_lo = sb("xT_lo", [P, 2, TG, KD, P], F16)
        logits = sb("logits", [P, TG, E])
        top = sb("top", [P, TG, 8])
        top_at = sb("top_at", [P, TG, 8], U32)
        is_top = sb("is_top", [P, 2, TG, E])
        kept = sb("kept", [P, TG, E])
        below = sb("below", [P, TG, E])
        expd = sb("expd", [P, TG, E])
        gz = sb("gz", [P, TG, E])
        gsum = sb("gsum", [P, TG])
        grec = sb("grec", [P, TG])
        gates = sb("gates", [P, P])
        gscaled = sb("gscaled", [P, 2, TG, E])
        gT = sb("gT", [P, P])
        acc = sb("acc", [P, 2, D])
        part = sb("part", [P, 2, 4, D])
        pair = sb("pair", [P, 2, 2, D])
        rest = sb("rest", [P, 2, D])

        w_loaded = sem("w_loaded")
        zeroed = sem("zeroed")
        const_ready = sem("const_ready")
        wmax_ready = sem("wmax_ready")
        wmax_all_ready = sem("wmax_all_ready")
        prep_step = sem("prep_step")
        w_ready = sem("w_ready")
        stats_ready = sem("stats_ready")
        mv_ready = sem("mv_ready")
        var_ready = sem("var_ready")
        rstd_ready = sem("rstd_ready")
        xn_ready = sem("xn_ready")
        xT_done = sem("xT_done")
        hi_ready = sem("hi_ready")
        lo_ready = sem("lo_ready")
        logits_done = sem("logits_done")
        gate_step = sem("gate_step")
        below_ready = sem("below_ready")
        gate_mass = sem("gate_mass")
        rec_ready = sem("rec_ready")
        exp_ready = sem("exp_ready")
        gates_ready = sem("gates_ready")
        gT_done = sem("gT_done")
        gT_ready = sem("gT_ready")
        bank_done = sem("bank_done")
        vector_free = sem("vector_free")
        scalar_free = sem("scalar_free")
        bias_done = sem("bias_done")
        acc_step = sem("acc_step")
        pair_ready = sem("pair_ready")
        rest_ready = sem("rest_ready")
        tile_done = sem("tile_done")
        stored = sem("stored")
        vector_passed = sem("vector_passed")
        pool_passed = sem("pool_passed")

        ORDER = (0, 2, 1, 3)

        def pipelined(eng, group):
            with eng.Fori(0, NG // 2 - 1) as i:
                group(i * 2, 0, False)
                group(i * 2 + 1, 1, False)
            group(NG - 2, 0, False)
            group(NG - 1, 1, True)

        with nc.Block() as block:
            @block.sync
            def _(sp):
                sp.dma_start(w32[:, :, :, :], C.expert_w.rearrange("(k p) e o -> p k e o", p=P)).then_inc(w_loaded, 16)
                sp.dma_start(gw32[:, :, :], C.gate_wT.rearrange("(k p) e -> p k e", p=P)).then_inc(w_loaded, 16)
                sp.dma_start(gate_b[:, :, :], C.gate_b.rearrange("(a b e) -> a b e", a=1, b=1)
                             .broadcast_to([P, TG, E])).then_inc(w_loaded, 16)
                sp.wait_ge(zeroed, 1)
                for j in range(TG):
                    sp.dma_start(eb_rows[E * j:E * (j + 1), j, :], C.expert_b).then_inc(w_loaded, 16)
                if out_dram is not None:
                    with sp.Fori(0, NG) as g:
                        sp.wait_ge(tile_done, g * TG + TG)
                        sp.dma_start(out_dram[:, bass.ds(g * TG, TG), :],
                                     xres[:, bass.ds(g * TG, TG), :]).then_inc(stored, 16)
                    sp.wait_ge(stored, 16 * NG)

            @block.gpsimd
            def _(pool):
                pool.memset(eb_rows[:, :, :], 0.0).then_inc(zeroed, 1)
                pool.memset(gates[:, :], 0.0).then_inc(const_ready, 1)
                pool.memset(mhalf[:, :], -0.5).then_inc(const_ready, 1)
                pool.iota(iota8[:, :, :], pattern=[[0, TG], [1, E]], base=0, channel_multiplier=0,
                          allow_small_or_imprecise_dtypes=True).then_inc(const_ready, 1)
                pool.wait_ge(wmax_ready, 2)
                pool.partition_all_reduce(wmax_all[:, :], wmax[:, :], P, RMAX).then_inc(wmax_all_ready, 1)

                def rstd_of(G):
                    wait_alone(pool, mv_ready, G * TG + TG, pool_passed)
                    pool.tensor_scalar(var_eps[:, :], mv[:, :, 1], EPS, LN_SCALE ** -2, ALU.add,
                                       ALU.mult).then_inc(var_ready, 1)
                    pool.wait_ge(var_ready, G + 1)
                    pool.tensor_tensor(rstd[:, :], var_eps[:, :], mhalf[:, :], ALU.pow).then_inc(rstd_ready, 1)

                def sum_parts(G, j):
                    b = j % 2
                    T = G * TG + j
                    pool.wait_ge(scalar_free, T * 4 + 8)
                    pool.tensor_tensor(pair[:, b, :, :], part[:, b, 0:2, :], part[:, b, 2:4, :], ALU.add).then_inc(pair_ready, 1)
                    pool.wait_ge(pair_ready, T + 1)
                    pool.tensor_tensor(rest[:, b, :], pair[:, b, 0, :], pair[:, b, 1, :], ALU.add).then_inc(rest_ready, 1)

                pool.wait_ge(const_ready, 3)
                rstd_of(0)

                def group(G, par, last):
                    if not last:
                        rstd_of(G + 1)
                    for j in range(TG):
                        sum_parts(G, j)

                pipelined(pool, group)

            @block.scalar
            def _(act):
                def split_hi(G, par):
                    for h in range(2):
                        act.wait_ge(xT_done, G * 2 + h + 1)
                        act.activation(xT_hi[:, par, 2 * h:2 * h + 2, :, :],
                                       xT_ps[h][:, :].rearrange("p (t k c) -> p t k c", t=2, k=KD),
                                       ACT.Copy).then_inc(hi_ready, 1)

                def exp_gates(G):
                    act.wait_ge(below_ready, G + 1)
                    act.activation(expd[:, :, :], below[:, :, :], ACT.Exp).then_inc(exp_ready, 1)

                def take_gT(G):
                    act.wait_ge(gT_done, G + 1)
                    act.activation(gT[:, :], gT_ps, ACT.Copy).then_inc(gT_ready, 1)

                def gated_parts(G, par, j):
                    T = G * TG + j
                    for n in (2, 3):
                        act.wait_ge(bank_done, T * 4 + ORDER.index(n) + 1)
                        if n == 2:
                            act.wait_ge(gates_ready, G * 2 + 2)
                            act.wait_ge(rest_ready, T + 1)
                        for h in range(2):
                            e = 2 * n + h
                            act.activation(part[:, j % 2, e - 4, :], main[n][:, h * D:(h + 1) * D], ACT.Copy,
                                           scale=gscaled[:, par, j, e:e + 1]).then_inc(scalar_free, 1)

                act.sem_inc(rest_ready, 2)
                act.sem_inc(scalar_free, 4)
                split_hi(0, 0)
                exp_gates(0)

                def group(G, par, last):
                    take_gT(G)
                    gated_parts(G, par, 0)
                    if not last:
                        split_hi(G + 1, 1 - par)
                    gated_parts(G, par, 1)
                    if not last:
                        exp_gates(G + 1)
                    gated_parts(G, par, 2)
                    gated_parts(G, par, 3)

                pipelined(act, group)

            @block.vector
            def _(dve):
                dve.sem_inc(vector_free, 4)
                dve.sem_inc(acc_step, 1)
                dve.wait_ge(w_loaded, 16 * (3 + TG))
                dve.tensor_reduce(wmax[:, 0:1], w32[:, :, :, :], AX.XYZ, ALU.max,
                                  apply_absolute_value=True).then_inc(wmax_ready, 1)
                dve.tensor_reduce(wmax[:, 1:2], gw32[:, :, :], AX.XY, ALU.max,
                                  apply_absolute_value=True).then_inc(wmax_ready, 1)
                dve.wait_ge(wmax_all_ready, 1)
                dve.tensor_scalar(wmax_all[:, :], wmax_all[:, :], 1e-30, 1e30, ALU.max, ALU.min).then_inc(prep_step, 1)
                dve.wait_ge(prep_step, 1)
                dve.reciprocal(scale[:, :], wmax_all[:, :]).then_inc(prep_step, 1)
                dve.wait_ge(prep_step, 2)
                dve.tensor_scalar(scale[:, :].bitcast(I32), scale[:, :].bitcast(I32), 0x7F800000, None,
                                  ALU.bitwise_and).then_inc(prep_step, 1)
                dve.wait_ge(prep_step, 3)
                dve.tensor_scalar(scale[:, :], scale[:, :], W_TOP, None, ALU.mult).then_inc(prep_step, 1)
                dve.wait_ge(prep_step, 4)
                dve.reciprocal(unscale[:, :], scale[:, :]).then_inc(prep_step, 1)
                dve.wait_ge(prep_step, 5)
                dve.tensor_scalar(unscale[:, :], unscale[:, :], 1.0 / LN_SCALE, None, ALU.mult).then_inc(prep_step, 1)
                step = 6
                for k in range(KD):
                    w = w32[:, k, :, :].rearrange("p e o -> p (e o)")
                    dve.wait_ge(prep_step, step)
                    dve.tensor_scalar(wprod[:, :], w, scale[:, 0:1], None, ALU.mult).then_inc(prep_step, 1)
                    dve.wait_ge(prep_step, step + 1)
                    dve.tensor_copy(w_hi[:, k, :], wprod[:, :]).then_inc(prep_step, 1)
                    dve.wait_ge(prep_step, step + 2)
                    dve.tensor_tensor(w_lo[:, k, :], wprod[:, :], w_hi[:, k, :], ALU.subtract).then_inc(prep_step, 1)
                    step += 3
                dve.tensor_scalar(gw_hi[:, :, :], gw32[:, :, :], scale[:, 1:2], None, ALU.mult).then_inc(prep_step, 1)
                dve.wait_ge(prep_step, step + 1)
                dve.scalar_tensor_tensor(gw_lo[:, :, :], gw32[:, :, :], scale[:, 1:2], gw_hi[:, :, :], ALU.mult,
                                         ALU.subtract).then_inc(w_ready, 1)
                dve.wait_ge(const_ready, 3)

                def layernorm(G):
                    for j in range(TG):
                        dve.bn_stats(stats[:, j, :], xres[:, bass.ds(G * TG + j, 1), :].rearrange("p a d -> p (a d)")
                                     ).then_inc(stats_ready, 1)
                    wait_alone(dve, stats_ready, G * TG + TG, vector_passed)
                    for j in range(TG):
                        dve.bn_aggr(mv[:, j, :], stats[:, j, :]).then_inc(mv_ready, 1)
                    dve.wait_ge(rstd_ready, G + 1)
                    for j in range(TG):
                        dve.tensor_scalar(xn[:, j, :], xres[:, bass.ds(G * TG + j, 1), :].rearrange("p a d -> p (a d)"),
                                          mv[:, j, 0:1], rstd[:, j:j + 1], ALU.subtract, ALU.mult).then_inc(xn_ready, 1)

                def split_lo(G, par):
                    for h in range(2):
                        dve.wait_ge(hi_ready, G * 2 + h + 1)
                        dve.tensor_tensor(xT_lo[:, par, 2 * h:2 * h + 2, :, :],
                                          xT_ps[h][:, :].rearrange("p (t k c) -> p t k c", t=2, k=KD),
                                          xT_hi[:, par, 2 * h:2 * h + 2, :, :], ALU.subtract).then_inc(lo_ready, 1)

                GS = 2 * TG + 3

                def gates_before_exp(G):
                    dve.wait_ge(logits_done, G + 1)
                    dve.scalar_tensor_tensor(logits[:, :, :], logit_ps, unscale[:, 1:2], gate_b[:, :, :], ALU.mult,
                                             ALU.add).then_inc(gate_step, 1)
                    wait_alone(dve, gate_step, G * GS + 1, vector_passed)
                    for j in range(TG):
                        dve.max(top[:, j, :], logits[:, j, :]).then_inc(gate_step, 1)
                    dve.wait_ge(gate_step, G * GS + 1 + TG)
                    dve.tensor_tensor(below[:, :, :], logits[:, :, :], top[:, :, 0:1].broadcast_to([P, TG, E]),
                                      ALU.subtract).then_inc(below_ready, 1)
                    for j in range(TG):
                        dve.max_index(top_at[:, j, :], top[:, j, :], logits[:, j, :]).then_inc(gate_step, 1)
                    dve.wait_ge(gate_step, G * GS + 1 + 2 * TG)
                    for m in range(2):
                        dve.tensor_tensor(is_top[:, m, :, :], iota8[:, :, :],
                                          top_at[:, :, m:m + 1].broadcast_to([P, TG, E]), ALU.is_equal).then_inc(gate_step, 1)

                def gates_after_exp(G, par):
                    dve.wait_ge(gate_step, G * GS + GS)
                    dve.tensor_tensor(kept[:, :, :], is_top[:, 0, :, :], is_top[:, 1, :, :], ALU.add).then_inc(gate_mass, 1)
                    dve.wait_ge(gate_mass, G * 3 + 1)
                    dve.wait_ge(exp_ready, G + 1)
                    dve.tensor_tensor(gz[:, :, :], expd[:, :, :], kept[:, :, :], ALU.mult).then_inc(gate_mass, 1)
                    dve.wait_ge(gate_mass, G * 3 + 2)
                    dve.tensor_reduce(gsum[:, :], gz[:, :, :], AX.X, ALU.add).then_inc(gate_mass, 1)
                    dve.wait_ge(gate_mass, G * 3 + 3)
                    dve.reciprocal(grec[:, :], gsum[:, :]).then_inc(rec_ready, 1)
                    dve.wait_ge(rec_ready, G + 1)
                    gv = gates[:, 0:TG * E].rearrange("p (t e) -> p t e", t=TG)
                    dve.tensor_tensor(gv, gz[:, :, :], grec[:, :].unsqueeze(2).broadcast_to([P, TG, E]),
                                      ALU.mult).then_inc(gates_ready, 1)
                    dve.wait_ge(gates_ready, G * 2 + 1)
                    dve.tensor_scalar(gscaled[:, par, :, :], gv, unscale[:, 0:1], None, ALU.mult).then_inc(gates_ready, 1)

                def combine(G, par, j):
                    T = G * TG + j
                    x_tile = xres[:, bass.ds(T, 1), :].rearrange("p a d -> p (a d)")
                    b = j % 2
                    if j == 0:
                        dve.wait_ge(gates_ready, G * 2 + 2)
                    for e in range(4):
                        n, h = e // 2, e % 2
                        if h == 0:
                            dve.wait_ge(bank_done, T * 4 + ORDER.index(n) + 1)
                        if e:
                            dve.wait_ge(vector_free, T * 4 + e + 4)
                        dve.scalar_tensor_tensor(acc[:, b, :], main[n][:, h * D:(h + 1) * D],
                                                 gscaled[:, par, j, e:e + 1], acc[:, b, :] if e else x_tile,
                                                 ALU.mult, ALU.add).then_inc(vector_free, 1)
                    dve.wait_ge(bias_done, T + 1)
                    dve.wait_ge(vector_free, T * 4 + 8)
                    dve.tensor_tensor(acc[:, b, :], acc[:, b, :], bias_ps[:, 0:D], ALU.add).then_inc(acc_step, 1)
                    dve.wait_ge(acc_step, T + 2)
                    dve.wait_ge(rest_ready, T + 3)
                    dve.tensor_tensor(x_tile, acc[:, b, :], rest[:, b, :], ALU.add).then_inc(tile_done, 1)

                layernorm(0)
                split_lo(0, 0)
                gates_before_exp(0)
                gates_after_exp(0, 0)

                def group(G, par, last):
                    if not last:
                        layernorm(G + 1)
                    combine(G, par, 0)
                    if not last:
                        split_lo(G + 1, 1 - par)
                    combine(G, par, 1)
                    if not last:
                        gates_before_exp(G + 1)
                    combine(G, par, 2)
                    if not last:
                        gates_after_exp(G + 1, 1 - par)
                    combine(G, par, 3)

                pipelined(dve, group)

            @block.tensor
            def _(pe):
                def turn(G):
                    for j in range(TG):
                        pe.wait_ge(xn_ready, G * TG + j + 1)
                        for k in range(KD):
                            at = (j % 2) * KD * P + k * P
                            ins = pe.transpose(xT_ps[j // 2][:, at:at + P], xn[:, j, k * P:(k + 1) * P], ident[:, :])
                        if j % 2:
                            ins.then_inc(xT_done, 1)

                def gate_logits(G, par):
                    for j in range(TG):
                        if j % 2 == 0:
                            pe.wait_ge(lo_ready, G * 2 + j // 2 + 1)
                        n = 0
                        for k in range(KD):
                            for xs, ws in ((xT_hi, gw_hi), (xT_hi, gw_lo), (xT_lo, gw_hi)):
                                ins = pe.matmul(logit_ps[:, j, :], xs[:, par, j, k, :], ws[:, k, :],
                                                start=(n == 0), stop=(n == 3 * KD - 1))
                                n += 1
                    ins.then_inc(logits_done, 1)

                def turn_gates(G):
                    pe.wait_ge(gates_ready, G * 2 + 1)
                    pe.transpose(gT_ps, gates[:, :], ident[:, :]).then_inc(gT_done, 1)

                def experts(G, par, j):
                    T = G * TG + j
                    for at, n in enumerate(ORDER):
                        if n < 2:
                            pe.wait_ge(vector_free, T * 4 + 2 * n + 2)
                        else:
                            pe.wait_ge(scalar_free, T * 4 + 2 * (n - 2) + 2)
                        m = 0
                        for k in range(KD):
                            for xs, ws in ((xT_hi, w_hi), (xT_hi, w_lo), (xT_lo, w_hi)):
                                ins = pe.matmul(main[n][:, :], xs[:, par, j, k, :], ws[:, k, n * 512:(n + 1) * 512],
                                                start=(m == 0), stop=(m == 3 * KD - 1))
                                m += 1
                        ins.then_inc(bank_done, 1)
                        if at == 1:
                            if j == 0:
                                pe.wait_ge(gT_ready, G + 1)
                            pe.wait_ge(acc_step, T + 1)
                            pe.matmul(bias_ps[:, 0:D], gT[:, :], eb_rows[:, j, :], start=True,
                                      stop=True).then_inc(bias_done, 1)

                pe.wait_ge(w_ready, 1)
                pe.wait_ge(w_loaded, 16 * (3 + TG))
                turn(0)
                gate_logits(0, 0)

                def group(G, par, last):
                    turn_gates(G)
                    experts(G, par, 0)
                    if not last:
                        turn(G + 1)
                    experts(G, par, 1)
                    if not last:
                        gate_logits(G + 1, 1 - par)
                    experts(G, par, 2)
                    experts(G, par, 3)

                pipelined(pe, group)


class Shared:
    pass


def bass_program(nc, x, q_wT, k_wT, v_wT, o_wT, dw_r, pw_rT, dw_i, pw_iT, a_gate_wT, alpha_raw, w_in, b_in, w_out, b_out,
                 rel_emb, gate_wT, gate_b, expert_w, expert_b, dft, idft_high, idft_low, mask, out):
    C = Shared()
    B, S, D = x.shape
    C.B, C.S, C.D = B, S, D
    C.NT = B * S // P
    C.CH, C.LOW, C.TAPS = 64, 4, dw_r.shape[2]
    C.NRE, C.NIM = C.CH // 2 + 1 - C.LOW, C.CH // 2 - C.LOW
    C.HD, C.NKV = 64, k_wT.shape[1] // 64
    C.q_wT, C.k_wT, C.v_wT, C.o_wT, C.a_gate_wT, C.alpha_raw = q_wT, k_wT, v_wT, o_wT, a_gate_wT, alpha_raw
    C.dw, C.pwT = (dw_r, dw_i), (pw_rT, pw_iT)
    C.dft, C.idft_high, C.idft_low, C.mask = dft, idft_high, idft_low, mask
    C.H = rel_emb.shape[1]
    C.w_in, C.b_in, C.w_out, C.b_out, C.rel_emb = w_in, b_in, w_out, b_out, rel_emb
    C.E, C.TG = gate_b.shape[0], 4
    C.gate_wT, C.gate_b, C.expert_w, C.expert_b = gate_wT, gate_b, expert_w, expert_b

    x_rows = x.flatten_outer_dims().rearrange("(t p) d -> p t d", p=P)
    out_rows = out.flatten_outer_dims().rearrange("(t p) d -> p t d", p=P)
    with ExitStack() as ctx:
        C.xres = ctx.enter_context(nc.sbuf_tensor("xres", [P, C.NT, D], F32))
        C.ident = ctx.enter_context(nc.sbuf_tensor("ident", [P, P], F32))
        x_loaded = ctx.enter_context(nc.semaphore("x_loaded"))
        ident_step = ctx.enter_context(nc.semaphore("ident_step"))
        with nc.Block() as block:
            @block.sync
            def _(sp):
                sp.dma_start(C.xres[:, :, :], x_rows).then_inc(x_loaded, 16)
                sp.wait_ge(x_loaded, 16)

            @block.gpsimd
            def _(pool):
                pool.memset(C.ident[:, :], 0.0).then_inc(ident_step, 1)
                pool.wait_ge(ident_step, 1)
                pool.affine_select(out=C.ident[:, :], in_=C.ident[:, :], compare_op=ALU.not_equal, fill=1.0, base=0,
                                   pattern=[[-1, P]], channel_multiplier=1).then_inc(ident_step, 1)
        spectral_layer(nc, C)
        token_ffn(nc, C, "_f1", None)
        position_attention(nc, C)
        token_ffn(nc, C, "_f2", out_rows)


_A, _B, _F = 'L0_attn_a_', 'L0_attn_b_', 'L0_ffn_'
_INS = [('x', _A + 'hidden_states', None), ('qw', _A + 'q_w', (1, 0)), ('kw', _A + 'k_w', (1, 0)), ('vw', _A + 'v_w', (1, 0)),
        ('ow', _A + 'o_w', (1, 0)), ('dwr', _A + 'dw_r', None), ('pwr', _A + 'pw_r', (1, 0)), ('dwi', _A + 'dw_i', None),
        ('pwi', _A + 'pw_i', (1, 0)), ('agw', _A + 'gate_w', (1, 0)), ('alpha', _A + 'alpha_raw', None),
        ('w_in', _B + 'W_in', None), ('b_in', _B + 'b_in', None), ('w_out', _B + 'W_out', None), ('b_out', _B + 'b_out', None),
        ('rel_emb', _B + 'rel_emb', None),
        ('fgw', _F + 'gate_w', (1, 0)), ('fgb', _F + 'gate_b', None), ('few', _F + 'expert_w', (1, 0, 2)),
        ('feb', _F + 'expert_b', None),
        ('dft', None, None), ('idh', None, None), ('idl', None, None), ('mask', None, None)]
_OUTS = [((16, 512, 256), 'float32')]


def fourier_constants():
    import numpy as _np

    CH, LOW, ROWS = 64, 4, 128
    n = _np.arange(CH)[:, None]
    k = _np.arange(CH // 2 + 1)[None, :]
    ang = 2 * _np.pi * ((n * k) % CH) / CH
    fwd_re, fwd_im = _np.cos(ang), -_np.sin(ang)
    fwd_im[:, 0] = fwd_im[:, CH // 2] = 0.0
    weight = _np.where((k == 0) | (k == CH // 2), 1.0, 2.0) / CH
    inv_re, inv_im = (fwd_re * weight).T, (fwd_im * weight).T
    NRE, NIM = CH // 2 + 1 - LOW, CH // 2 - LOW
    dft = _np.zeros((ROWS, 4 * LOW + 2 * (NRE + NIM)))
    high = _np.zeros((ROWS, ROWS))
    low = _np.zeros((8, ROWS, ROWS))
    for c in range(2):
        t = slice(CH * c, CH * (c + 1))
        dft[t, LOW * c:LOW * (c + 1)] = fwd_re[:, :LOW]
        dft[t, LOW * (2 + c):LOW * (3 + c)] = fwd_im[:, :LOW]
        re0, im0 = c * NRE, 2 * NRE + c * NIM
        dft[t, 4 * LOW + re0:4 * LOW + re0 + NRE] = fwd_re[:, LOW:]
        dft[t, 4 * LOW + im0:4 * LOW + im0 + NIM] = fwd_im[:, LOW:CH // 2]
        high[re0:re0 + NRE, t] = inv_re[LOW:]
        high[im0:im0 + NIM, t] = inv_im[LOW:CH // 2]
        for tile in range(8):
            r = 64 * (tile // 4) + LOW * (2 * (tile % 4) + c)
            low[tile, r:r + LOW, t] = inv_re[:LOW]
            low[tile, r + 32:r + 32 + LOW, t] = inv_im[:LOW]
    row = _np.arange(ROWS)
    seq, chunk = row // 32, row % 32 // LOW
    barred = (seq[:, None] != seq[None, :]) | (chunk[:, None] < chunk[None, :])
    mask = _np.where(barred, 1e30, 0.0)
    return {"dft": dft, "idh": high, "idl": low, "mask": mask}
_OUTS = [((16, 512, 256), 'float32')]


def kernel(**inputs):
    import numpy as _np
    import concourse.bacc as _bacc
    from concourse import mybir as _mybir
    from concourse.bass_utils import run_bass_kernel_spmd as _run

    nc = _bacc.Bacc("TRN2", target_bir_lowering=False, num_devices=1)
    arrays, args, constants = {}, [], fourier_constants()
    for name, source, axes in _INS:
        a = _np.asarray(inputs[source]) if source else constants[name].astype(_np.float32)
        a = _np.ascontiguousarray(a if axes is None else a.transpose(axes))
        arrays[f"in_{name}_dram"] = a
        args.append(nc.dram_tensor(f"in_{name}_dram", a.shape, _mybir.dt.from_np(a.dtype), kind="ExternalInput").ap())
    for i, (shape, dtype) in enumerate(_OUTS):
        dt = _mybir.dt.from_np(_np.dtype(dtype))
        args.append(nc.dram_tensor(f"out_{i}_dram", shape, dt, kind="ExternalOutput").ap())
    bass_program(nc, *args)
    r = _run(nc, [arrays], core_ids=[0])
    got = tuple(r.results[0][f"out_{i}_dram"] for i in range(len(_OUTS)))
    return got[0]
```

```python
from contextlib import ExitStack

import concourse.bass as bass
from concourse import mybir

F32 = mybir.dt.float32
F16 = mybir.dt.float16
BF16 = mybir.dt.bfloat16
I32 = mybir.dt.int32
U32 = mybir.dt.uint32
ALU = mybir.AluOpType
ACT = mybir.ActivationFunctionType
AX = mybir.AxisListType
RMAX = bass.bass_isa.ReduceOp.max

P = 128
EPS = 1e-5
LN_SCALE = 1024.0
W_TOP = 2.0 ** 14


def wait_alone(eng, sem, value, passed):
    eng.wait_ge(sem, value)
    eng.sem_inc(passed, 1)


def need(eng, s, value):
    if not (isinstance(value, int) and value <= 0):
        eng.wait_ge(s, value)


def need_alone(eng, sem, value, passed):
    if not (isinstance(value, int) and value <= 0):
        wait_alone(eng, sem, value, passed)


def spectral_layer(nc, C):
    with ExitStack() as outer:
        C.xlow = outer.enter_context(nc.sbuf_tensor("a_xlow", [P, C.D // P, C.B, 2, C.S // C.CH * C.LOW], F32))
        load_mix, load_attend = mix_weights(nc, C, outer), attend_weights(nc, C, outer)
        with ExitStack() as ctx:
            kd, nch = C.D // P, C.B * C.S // C.CH
            C.x_re = ctx.enter_context(nc.sbuf_tensor("a_x_re", [P, kd, nch, C.TAPS - 1 + C.NRE], F32))
            C.x_im = ctx.enter_context(nc.sbuf_tensor("a_x_im", [P, kd, nch, C.TAPS - 1 + C.NIM], F32))
            C.gT = ctx.enter_context(nc.sbuf_tensor("a_gT", [P, C.D // P, C.B * C.S // C.CH], F32))
            transform(nc, C, (load_mix, load_attend))
            mix_high(nc, C)
        attend_low(nc, C)


def transform(nc, C, loads_ahead):
    D, B, S, CH, LOW, TAPS, NRE, NIM = C.D, C.B, C.S, C.CH, C.LOW, C.TAPS, C.NRE, C.NIM
    KD = D // P
    TG = S // P
    NC2 = P // CH
    NCH = B * S // CH
    LC = 2 * NC2 * LOW
    xres, ident, xlow, x_re, x_im = C.xres, C.ident, C.xlow, C.x_re, C.x_im
    with ExitStack() as ctx:
        def sb(name, shape, dt=F32):
            return ctx.enter_context(nc.sbuf_tensor(f"t_{name}", shape, dt))

        def sem(name):
            return ctx.enter_context(nc.semaphore(f"t_{name}"))

        dft_ps = [ctx.enter_context(nc.psum_tensor(f"t_dft_ps{n}", [P, KD, 256], F32)) for n in range(4)]
        gate_ps = ctx.enter_context(nc.psum_tensor("t_gate_ps", [P, KD, NCH], F32))
        NF = LC + NC2 * (NRE + NIM)
        dft = sb("dft", [P, NF])
        gate_wT = sb("gate_wT", [P, KD, D])
        stats = sb("stats", [P, TG, 6])
        mv = sb("mv", [P, TG, 2])
        var_eps = sb("var_eps", [P, TG])
        rstd = sb("rstd", [P, TG])
        mhalf = sb("mhalf", [P, TG])
        xn = sb("xn", [P, 2, TG, D])
        eg = sb("eg", [P, KD, NCH])

        x_in = [sem(f"x_in{n}") for n in range(2)]
        loaded = sem("loaded")
        ident_step = sem("ident_step")
        const_ready = sem("const_ready")
        stats_ready = sem("stats_ready")
        mv_ready = sem("mv_ready")
        var_ready = sem("var_ready")
        rstd_ready = sem("rstd_ready")
        xn_ready = sem("xn_ready")
        added = sem("added")
        dft_done = sem("dft_done")
        act_took = sem("act_took")
        dve_took = sem("dve_took")
        gate_done = sem("gate_done")
        exp_ready = sem("exp_ready")
        gate_step = sem("gate_step")
        v_passed, p_passed = C.vector_passed, C.pool_passed

        def all_batches(eng, group):
            group(0, 0, False)
            group(0, 1, False)
            with eng.Fori(1, B // 2 - 1) as i:
                group(i, 0, False)
                group(i, 1, False)
            group(B // 2 - 1, 0, False)
            group(B // 2 - 1, 1, True)

        def take(eng, b, j, took):
            at = LC + NC2 * NRE
            eng.wait_ge(dft_done, b * TG + j + 1)
            for out, lo, hi, nf in (
                    (xlow[:, :, bass.ds(b, 1), :, j * NC2 * LOW:(j + 1) * NC2 * LOW].rearrange("p k a r f -> p k (a r) f"),
                     0, LC, NC2 * LOW),
                    (x_re[:, :, bass.ds(b * (TG * NC2) + j * NC2, NC2), TAPS - 1:], LC, at, NRE),
                    (x_im[:, :, bass.ds(b * (TG * NC2) + j * NC2, NC2), TAPS - 1:], at, NF, NIM)):
                src = dft_ps[j][:, :, lo:hi].rearrange("p k (c f) -> p k c f", f=nf)
                if took is act_took:
                    eng.activation(out, src, ACT.Copy).then_inc(took, 1)
                else:
                    eng.tensor_copy(out, src).then_inc(took, 1)

        with nc.Block() as block:
            @block.sync
            def _(sp):
                def load_x(b, par):
                    sp.dma_start(xres[:, bass.ds(b * TG, TG), :], C.x_rows[:, bass.ds(b * TG, TG), :]).then_inc(x_in[par], 16)

                load_x(0, 0)
                sp.dma_start(dft[:, :], C.dft).then_inc(loaded, 16)
                load_x(1, 1)
                sp.dma_start(gate_wT[:, :, :], C.a_gate_wT.rearrange("(k p) e -> p k e", p=P)).then_inc(loaded, 16)
                with sp.Fori(1, B // 2) as i:
                    for par in range(2):
                        sp.wait_ge(x_in[par], i * 16)
                        load_x(i * 2 + par, par)
                for load in loads_ahead:
                    load(sp)

            @block.gpsimd
            def _(pool):
                pool.memset(ident[:, :], 0.0).then_inc(ident_step, 1)
                pool.wait_ge(ident_step, 1)
                pool.affine_select(out=ident[:, :], in_=ident[:, :], compare_op=ALU.not_equal, fill=1.0, base=0,
                                   pattern=[[-1, P]], channel_multiplier=1).then_inc(ident_step, 1)
                pool.wait_ge(ident_step, 2)
                pool.memset(mhalf[:, :], -0.5).then_inc(const_ready, 1)
                pool.memset(x_re[:, :, :, 0:TAPS - 1], 0.0).then_inc(const_ready, 1)
                pool.memset(x_im[:, :, :, 0:TAPS - 1], 0.0).then_inc(const_ready, 1)
                pool.wait_ge(const_ready, 3)

                def rstd_of(b):
                    wait_alone(pool, mv_ready, b * TG + TG, p_passed)
                    pool.tensor_scalar(var_eps[:, :], mv[:, :, 1], EPS, None, ALU.add).then_inc(var_ready, 1)
                    pool.wait_ge(var_ready, b + 1)
                    pool.tensor_tensor(rstd[:, :], var_eps[:, :], mhalf[:, :], ALU.pow).then_inc(rstd_ready, 1)

                def group(i, par, last):
                    b = i * 2 + par
                    if not last:
                        rstd_of(b + 1)
                    pool.wait_ge(xn_ready, b * TG + TG)
                    rows = xres[:, bass.ds(b * TG, TG), :]
                    pool.tensor_tensor(rows, rows, xn[:, par, :, :], ALU.add).then_inc(added, 1)

                rstd_of(0)
                all_batches(pool, group)

            @block.scalar
            def _(act):
                def group(i, par, last):
                    b = i * 2 + par
                    for j in range(TG - 1):
                        take(act, b, j, act_took)

                all_batches(act, group)
                act.wait_ge(gate_done, 1)
                act.activation(eg[:, :, :], gate_ps[:, :, :], ACT.Exp, scale=-1.0 / CH).then_inc(exp_ready, 1)

            @block.vector
            def _(dve):
                def row_stats(i, par):
                    b = i * 2 + par
                    dve.wait_ge(x_in[par], i * 16 + 16)
                    for j in range(TG):
                        dve.bn_stats(stats[:, j, :], xres[:, bass.ds(b * TG + j, 1), :].rearrange("p a d -> p (a d)")
                                     ).then_inc(stats_ready, 1)
                    wait_alone(dve, stats_ready, b * TG + TG, v_passed)
                    for j in range(TG):
                        dve.bn_aggr(mv[:, j, :], stats[:, j, :]).then_inc(mv_ready, 1)

                def layernorm(i, par):
                    b = i * 2 + par
                    need(dve, dft_done, b * TG - TG)
                    need(dve, added, b - 1)
                    dve.wait_ge(rstd_ready, b + 1)
                    for j in range(TG):
                        dve.tensor_scalar(xn[:, par, j, :], xres[:, bass.ds(b * TG + j, 1), :].rearrange("p a d -> p (a d)"),
                                          mv[:, j, 0:1], rstd[:, j:j + 1], ALU.subtract, ALU.mult).then_inc(xn_ready, 1)

                def group(i, par, last):
                    b = i * 2 + par
                    if not last:
                        row_stats(i + par, 1 - par)
                    take(dve, b, TG - 1, dve_took)
                    if not last:
                        layernorm(i + par, 1 - par)

                row_stats(0, 0)
                layernorm(0, 0)
                all_batches(dve, group)
                dve.wait_ge(exp_ready, 1)
                dve.tensor_scalar(eg[:, :, :], eg[:, :, :], 1.0, None, ALU.add).then_inc(gate_step, 1)
                dve.wait_ge(gate_step, 1)
                dve.reciprocal(C.gT[:, :, :], eg[:, :, :]).then_inc(gate_step, 1)

            @block.tensor
            def _(pe):
                pe.wait_ge(loaded, 32)

                def group(i, par, last):
                    b = i * 2 + par
                    for j in range(TG):
                        pe.wait_ge(xn_ready, b * TG + j + 1)
                        if j < TG - 1:
                            need(pe, act_took, b * (3 * (TG - 1)) + (j + 2 - TG) * 3)
                        else:
                            need(pe, dve_took, b * 3)
                        for k in range(KD):
                            ins = pe.matmul(dft_ps[j][:, k, 0:NF], xn[:, par, j, k * P:(k + 1) * P], dft[:, :],
                                            start=True, stop=True)
                        ins.then_inc(dft_done, 1)

                all_batches(pe, group)
                pe.wait_ge(act_took, B * 3 * (TG - 1))
                pe.wait_ge(dve_took, B * 3)
                for o in range(KD):
                    for k in range(KD):
                        ins = pe.matmul(gate_ps[:, o, :], gate_wT[:, k, o * P:(o + 1) * P],
                                        xlow[:, k, :, 0, :].rearrange("p b (c f) -> p b c f", f=LOW)[:, :, :, 0],
                                        start=(k == 0), stop=(k == KD - 1))
                ins.then_inc(gate_done, 1)


def mix_weights(nc, C, ctx):
    KD = C.D // P
    C.taps = ctx.enter_context(nc.sbuf_tensor("h_taps", [P, 2, KD, C.TAPS], F32))
    C.mix_wT = ctx.enter_context(nc.sbuf_tensor("h_pwT", [P, 2, KD, C.D], F32))
    C.idft_sb = ctx.enter_context(nc.sbuf_tensor("h_idft", [P, P], F32))
    C.mix_loaded = ctx.enter_context(nc.semaphore("h_loaded"))

    def load(sp):
        for r in range(2):
            sp.dma_start(C.taps[:, r, :, :], C.dw[r].rearrange("(k p) o t -> p k (o t)", p=P)).then_inc(C.mix_loaded, 16)
            sp.dma_start(C.mix_wT[:, r, :, :], C.pwT[r].rearrange("(k p) e -> p k e", p=P)).then_inc(C.mix_loaded, 16)
        sp.dma_start(C.idft_sb[:, :], C.idft_high).then_inc(C.mix_loaded, 16)

    return load


def mix_high(nc, C):
    D, B, S, CH, TAPS, NRE, NIM = C.D, C.B, C.S, C.CH, C.TAPS, C.NRE, C.NIM
    KD = D // P
    TG = S // P
    NC2 = P // CH
    NB = S // CH
    RE, IM = NB * NRE, NB * NIM
    TR, TI = NC2 * NRE, NC2 * NIM
    xres, x_re, x_im, gT, ident = C.xres, C.x_re, C.x_im, C.gT, C.ident
    with ExitStack() as ctx:
        def sb(name, shape, dt=F32):
            return ctx.enter_context(nc.sbuf_tensor(f"h_{name}", shape, dt))

        def sem(name):
            return ctx.enter_context(nc.semaphore(f"h_{name}"))

        mix_ps = [ctx.enter_context(nc.psum_tensor(f"h_mix_ps{o}", [P, 512], F32)) for o in range(KD)]
        turn_ps = [ctx.enter_context(nc.psum_tensor(f"h_turn_ps{n}", [P, 2, KD, P], F32)) for n in range(2)]
        out_ps = [ctx.enter_context(nc.psum_tensor(f"h_out_ps{n}", [P, 2, D], F32)) for n in range(2)]
        taps, pwT, idft, loaded = C.taps, C.mix_wT, C.idft_sb, C.mix_loaded
        filt = sb("filt", [P, 2, KD, RE + IM])
        act_f = sb("act_f", [P, KD, RE + IM])
        product = sb("product", [P, TAPS - 1, IM])
        hT = sb("hT", [P, KD, TG, P])
        h = sb("h", [P, TG, KD, P])

        zeroed = sem("zeroed")
        tap0_done = sem("tap0_done")
        filt_step = sem("filt_step")
        product_ready = sem("product_ready")
        pool_step = sem("pool_step")
        act_done = sem("act_done")
        mixed = sem("mixed")
        gated = sem("gated")
        turned = sem("turned")
        h_ready = sem("h_ready")
        inverted = sem("inverted")
        added = sem("added")

        PIECES = [(k, r) for k in range(KD) for r in range(2)]
        NP_ = len(PIECES)
        NV = NP_ - 1
        STEPS = (TAPS - 1) * NV

        def columns(r):
            return (0, RE) if r == 0 else (RE, RE + IM)

        def pipelined(eng, slot):
            for i in range(2):
                slot(i, i, i)
            with eng.Fori(1, B // 2 - 1) as m:
                for par in range(2):
                    slot(m * 2 + par, None, par)
            for i in range(B - 2, B + 2):
                slot(i, i, i % 2)

        def piece(b, par, n, t):
            k, r = PIECES[n]
            lo, hi = columns(r)
            nf = (NRE, NIM)[r]
            return ((x_re, x_im)[r][:, k, bass.ds(b * NB, NB), t:t + nf],
                    filt[:, par, k, lo:hi].rearrange("p (c f) -> p c f", f=nf), taps[:, r, k, t:t + 1])

        def exists(at, delay):
            return at is None or 0 <= at - delay < B

        with nc.Block() as block:
            @block.gpsimd
            def _(pool):
                pool.memset(hT[:, :, :, TR + TI:], 0.0).then_inc(zeroed, 1)

                def slot(i, at, par):
                    if exists(at, 0):
                        pool.wait_ge(tap0_done, i * NP_ + NP_)
                        for t in range(1, TAPS):
                            src, acc, tap = piece(i, par, NV, t)
                            pool.wait_ge(product_ready, i * (TAPS - 1) + t)
                            if t > 1:
                                pool.wait_ge(pool_step, i * (TAPS - 1) + (t - 1))
                            pool.tensor_tensor(acc, acc, product[:, t - 1, :].rearrange("p (c f) -> p c f", f=NIM),
                                               ALU.add).then_inc(pool_step, 1)

                pipelined(pool, slot)

            @block.scalar
            def _(act):
                def first_tap(b, par, n):
                    src, acc, tap = piece(b, par, n, 0)
                    act.activation(acc, src, ACT.Copy, scale=tap).then_inc(tap0_done, 1)

                def products(b, par):
                    for t in range(1, TAPS):
                        src, acc, tap = piece(b, par, NV, t)
                        need(act, pool_step, b * (TAPS - 1) + (t + 1 - TAPS))
                        act.activation(product[:, t - 1, :].rearrange("p (c f) -> p c f", f=NIM), src, ACT.Copy,
                                       scale=tap).then_inc(product_ready, 1)

                def slot(i, at, par):
                    if at is None or at + 1 < B:
                        for n in range(NP_):
                            need(act, act_done, (i - 1) * NP_ + n + 1)
                            first_tap(i + 1, 1 - par, n)
                        products(i + 1, 1 - par)
                    if exists(at, 0):
                        for n, (k, r) in enumerate(PIECES):
                            lo, hi = columns(r)
                            if n < NV:
                                act.wait_ge(filt_step, i * STEPS + (STEPS - NV + n + 1))
                            else:
                                act.wait_ge(pool_step, i * (TAPS - 1) + (TAPS - 1))
                            if n == 0:
                                need(act, mixed, i * KD)
                            act.activation(act_f[:, k, lo:hi], filt[:, par, k, lo:hi], ACT.Gelu).then_inc(act_done, 1)
                    if exists(at, 1):
                        for n in range(2):
                            act.wait_ge(turned, i * 2 + (n - 1))
                            if n == 0:
                                need(act, inverted, i * 2 - 2)
                            act.activation(h[:, 2 * n:2 * n + 2, :, :], turn_ps[n][:, :, :, :], ACT.Copy).then_inc(h_ready, 1)

                act.wait_ge(loaded, 16 * 5)
                for n in range(NP_):
                    first_tap(0, 0, n)
                products(0, 0)
                pipelined(act, slot)

            @block.vector
            def _(dve):
                dve.wait_ge(loaded, 16 * 5)

                def filter_batch(b, par):
                    for t in range(1, TAPS):
                        for n in range(NV):
                            src, acc, tap = piece(b, par, n, t)
                            if t == 1:
                                dve.wait_ge(tap0_done, b * NP_ + n + 1)
                            else:
                                dve.wait_ge(filt_step, b * STEPS + ((t - 2) * NV + n + 1))
                            dve.scalar_tensor_tensor(acc, src, tap, acc, ALU.mult, ALU.add).then_inc(filt_step, 1)

                def gate_batch(i):
                    for o in range(KD):
                        dve.wait_ge(mixed, i * KD + (o + 1 - KD))
                        if o == 0:
                            need(dve, turned, i * 2 - 2)
                        for r in range(2):
                            lo, hi = columns(r)
                            nf = (NRE, NIM)[r]
                            t0 = (0, TR)[r]
                            g = gT[:, o, bass.ds(i * NB - NB, NB)].rearrange("p (t c) -> p t c", c=NC2)
                            dve.tensor_tensor(hT[:, o, :, t0:t0 + NC2 * nf].rearrange("p t (c f) -> p t c f", f=nf),
                                              mix_ps[o][:, lo:hi].rearrange("p (t c f) -> p t c f", c=NC2, f=nf),
                                              g.unsqueeze(3).broadcast_to([P, TG, NC2, nf]), ALU.mult).then_inc(gated, 1)

                def slot(i, at, par):
                    if exists(at, 0):
                        filter_batch(i, par)
                    if exists(at, 1):
                        gate_batch(i)
                    if exists(at, 2):
                        for n in range(2):
                            dve.wait_ge(inverted, i * 2 + (n - 3))
                            rows = xres[:, bass.ds(i * TG + (2 * n - 2 * TG), 2), :]
                            dve.tensor_tensor(rows, rows, out_ps[n][:, :, :], ALU.add).then_inc(added, 1)

                pipelined(dve, slot)

            @block.tensor
            def _(pe):
                pe.wait_ge(loaded, 16 * 5)
                pe.wait_ge(zeroed, 1)

                def slot(i, at, par):
                    if exists(at, 0):
                        pe.wait_ge(act_done, i * NP_ + NP_)
                        for o in range(KD):
                            need(pe, gated, i * (2 * KD) + (2 * o + 2 - 2 * KD))
                            for r in range(2):
                                lo, hi = columns(r)
                                for k in range(KD):
                                    ins = pe.matmul(mix_ps[o][:, lo:hi], pwT[:, r, k, o * P:(o + 1) * P], act_f[:, k, lo:hi],
                                                    start=(k == 0), stop=(k == KD - 1))
                            ins.then_inc(mixed, 1)
                    if exists(at, 1):
                        pe.wait_ge(gated, i * (2 * KD))
                        for n in range(2):
                            need(pe, h_ready, i * 2 + (n - 3))
                            for t in range(2):
                                for o in range(KD):
                                    ins = pe.transpose(turn_ps[n][:, t, o, :], hT[:, o, 2 * n + t, :], ident[:, :])
                            ins.then_inc(turned, 1)
                        for n in range(2):
                            pe.wait_ge(h_ready, i * 2 + (n - 1))
                            need(pe, added, i * 2 + (n - 3))
                            for t in range(2):
                                ins = pe.matmul(out_ps[n][:, t, :], idft[:, :], h[:, 2 * n + t, :, :].rearrange("p o c -> p (o c)"),
                                                start=True, stop=True)
                            ins.then_inc(inverted, 1)

                pipelined(pe, slot)


def attend_weights(nc, C, ctx):
    D, HD, NKV = C.D, C.HD, C.NKV
    KD = D // P
    NQ = C.q_wT.shape[1] // P

    def sb(name, shape):
        return ctx.enter_context(nc.sbuf_tensor(f"l_{name}", shape, F32))

    C.q_w_sb = sb("q_wT", [P, KD, NQ * P])
    C.k_w_sb = sb("k_wT", [P, KD, NKV, 2, HD])
    C.v_w_sb = sb("v_wT", [P, KD, NKV, 2, HD])
    C.o_w_sb = sb("o_wT", [P, NQ, D])
    C.idft_low_sb = sb("idft", [P, 2 * C.NT // C.B, P])
    C.mask_sb = sb("mask", [P, P])
    C.alpha_sb = sb("alpha_raw", [P, 1])
    C.attend_loaded = ctx.enter_context(nc.semaphore("l_loaded"))
    C.attend_loads = 16 * (5 + 4 * KD)

    def load(sp):
        done = C.attend_loaded
        sp.dma_start(C.q_w_sb[:, :, :], C.q_wT.rearrange("(k p) e -> p k e", p=P)).then_inc(done, 16)
        for w, src in ((C.k_w_sb, C.k_wT), (C.v_w_sb, C.v_wT)):
            for k in range(KD):
                for e in range(2):
                    sp.dma_start(w[:, k, :, e, :], src[k * P:(k + 1) * P, :].rearrange("p (j d) -> p j d", d=HD)
                                 ).then_inc(done, 16)
        sp.dma_start(C.o_w_sb[:, :, :], C.o_wT.rearrange("(m p) e -> p m e", p=P)).then_inc(done, 16)
        sp.dma_start(C.idft_low_sb[:, :, :], C.idft_low.rearrange("t p c -> p t c")).then_inc(done, 16)
        sp.dma_start(C.mask_sb[:, :], C.mask).then_inc(done, 16)
        sp.dma_start(C.alpha_sb[:, :], C.alpha_raw.unsqueeze(0).broadcast_to([P, 1])).then_inc(done, 16)

    return load


def attend_low(nc, C):
    D, B = C.D, C.B
    KD = D // P
    HD, NKV = C.HD, C.NKV
    REP = C.q_wT.shape[1] // (NKV * HD)
    NQ = REP * NKV * HD // P
    G = B // 2
    xres, ident = C.xres, C.ident
    with ExitStack() as ctx:
        def sb(name, shape, dt=F32):
            return ctx.enter_context(nc.sbuf_tensor(f"l_{name}", shape, dt))

        def sem(name):
            return ctx.enter_context(nc.semaphore(f"l_{name}"))

        ps = [ctx.enter_context(nc.psum_tensor(f"l_ps{n}", [P, 512], F32)) for n in range(8)]
        s_ps, t_ps, o_ps, proj_ps, out_ps = ps[0:2], ps[2:4], ps[4], ps[5], ps[6:8]

        q_wT, k_wT, v_wT, o_wT, idft, mask = C.q_w_sb, C.k_w_sb, C.v_w_sb, C.o_w_sb, C.idft_low_sb, C.mask_sb
        alpha_raw, loaded, LOADS = C.alpha_sb, C.attend_loaded, C.attend_loads
        neg_ident = sb("neg_ident", [P, P])
        alpha = sb("alpha", [P, 1])
        alpha_e = sb("alpha_e", [P, 1])
        alpha_d = sb("alpha_d", [P, 1])
        qT = sb("qT", [P, NQ, G, P])
        kT = sb("kT", [P, G, NKV, 2, P])
        v = sb("v", [P, G, NKV * 2 * HD])
        masked = sb("masked", [P, 2, REP, P])
        neg_max = sb("neg_max", [P, 2, REP])
        probs = sb("probs", [P, 2, REP, P])
        sums = sb("sums", [P, 2, REP])
        recip = sb("recip", [P, 2, REP])
        normed = sb("normed", [P, 2, REP, P])
        probsT = sb("probsT", [P, 2, REP, P])
        oT = sb("oT", [P, NQ, P])
        low = sb("low", [P, D])

        const_ready = sem("const_ready")
        alpha_step = sem("alpha_step")
        alpha_exp = sem("alpha_exp")
        proj_done = sem("proj_done")
        act_took = sem("act_took")
        dve_took = sem("dve_took")
        scored = sem("scored")
        masked_done = sem("masked_done")
        exp_done = sem("exp_done")
        recip_done = sem("recip_done")
        normed_done = sem("normed_done")
        turned = sem("turned")
        pt_ready = sem("pt_ready")
        weighed = sem("weighed")
        o_ready = sem("o_ready")
        mixed = sem("mixed")
        low_ready = sem("low_ready")
        inverted = sem("inverted")
        added = sem("added")
        v_passed = C.vector_passed

        def x_rows(k, g):
            return C.xlow[:, k, bass.ds(g * 2, 2), :, :].rearrange("p b r f -> p (b r f)")

        UNITS = ([("q", m, n) for n in range(2) for m in range(NQ)] + [("k", j, n) for n in range(2) for j in range(NKV)] +
                 [("v", 0, g) for g in range(G)])
        HG = G // 2

        def taken_count(parity, upto):
            return sum(2 if UNITS[n][0] == "k" else 1 for n in range(upto) if n % 2 == parity)

        def take_units(eng, parity, done):
            for n, (what, m, at) in enumerate(UNITS):
                if n % 2 != parity:
                    continue
                eng.wait_ge(proj_done, n + 1)
                src = ps[n % 8]
                if what == "q":
                    pairs = [(qT[:, m, HG * at:HG * (at + 1), :], src[:, :].rearrange("p (g c) -> p g c", c=P), -HD ** -0.5)]
                elif what == "k":
                    pairs = [(kT[HD * e:HD * (e + 1), HG * at:HG * (at + 1), m, e, :],
                              src[HD * e:HD * (e + 1), :].rearrange("p (g c) -> p g c", c=P), 1.0) for e in range(2)]
                else:
                    pairs = [(v[:, at, :], src[:, :], 1.0)]
                for out, in_, scale in pairs:
                    if parity == 0:
                        eng.activation(out, in_, ACT.Copy, scale=scale).then_inc(done, 1)
                    elif scale == 1.0:
                        eng.tensor_copy(out, in_).then_inc(done, 1)
                    else:
                        eng.tensor_scalar(out, in_, scale, None, ALU.mult).then_inc(done, 1)

        def all_groups(eng, group):
            for g in range(G + 2):
                group(g, g)

        def unit(g, at, j, delay):
            back = (delay - j + NKV - 1) // NKV if delay > j else 0
            if at is not None and not 0 <= at * NKV + j - delay < G * NKV:
                return None
            return g - back, j - delay + back * NKV

        with nc.Block() as block:
            @block.gpsimd
            def _(pool):
                pool.memset(kT[0:HD, :, :, 1, :], 0.0).then_inc(const_ready, 1)
                pool.memset(kT[HD:P, :, :, 0, :], 0.0).then_inc(const_ready, 1)
                pool.wait_ge(const_ready, 2)
                pool.tensor_scalar(neg_ident[:, :], ident[:, :], -1.0, None, ALU.mult).then_inc(const_ready, 1)

                def group(g, at):
                    for j in range(NKV):
                        u = unit(g, at, j, 1)
                        if u:
                            n = u[0] * NKV + u[1]
                            pool.wait_ge(recip_done, n + 1)
                            need(pool, turned, n - 1)
                            pool.tensor_tensor(normed[:, u[1] % 2, :, :], probs[:, u[1] % 2, :, :],
                                               recip[:, u[1] % 2, :].unsqueeze(2).broadcast_to([P, REP, P]),
                                               ALU.mult).then_inc(normed_done, 1)

                all_groups(pool, group)

            @block.scalar
            def _(act):
                act.wait_ge(loaded, LOADS)
                act.activation(alpha_e[:, :], alpha_raw[:, :], ACT.Exp, scale=-1.0).then_inc(alpha_exp, 1)
                take_units(act, 0, act_took)

                def group(g, at):
                    for j in range(NKV):
                        u = unit(g, at, j, 0)
                        if u:
                            n = u[0] * NKV + u[1]
                            act.wait_ge(masked_done, n * REP + REP)
                            need(act, normed_done, n - 1)
                            for h in range(REP):
                                act.activation(probs[:, j % 2, h, :], masked[:, j % 2, h, :], ACT.Exp, scale=-1.0,
                                               bias=neg_max[:, j % 2, h:h + 1],
                                               accum_out=sums[:, j % 2, h:h + 1]).then_inc(exp_done, 1)
                        u = unit(g, at, j, 2)
                        if u:
                            n = u[0] * NKV + u[1]
                            act.wait_ge(turned, n + 1)
                            need(act, weighed, n - 1)
                            act.activation(probsT[:, u[1] % 2, :, :], t_ps[u[1] % 2][:, :].rearrange("p (h c) -> p h c", c=P),
                                           ACT.Copy).then_inc(pt_ready, 1)
                    if at is None or 0 <= at - 1 < G:
                        act.wait_ge(mixed, g)
                        need(act, inverted, (g - 1) * NKV)
                        act.activation(low[:, :], proj_ps[:, 0:D], ACT.Copy, scale=alpha[:, 0:1]).then_inc(low_ready, 1)

                act.wait_ge(alpha_step, 2)
                all_groups(act, group)

            @block.vector
            def _(dve):
                dve.wait_ge(alpha_exp, 1)
                dve.tensor_scalar(alpha_d[:, :], alpha_e[:, :], 1.0, None, ALU.add).then_inc(alpha_step, 1)
                dve.wait_ge(alpha_step, 1)
                dve.reciprocal(alpha[:, :], alpha_d[:, :]).then_inc(alpha_step, 1)
                take_units(dve, 1, dve_took)

                def group(g, at):
                    for j in range(NKV):
                        u = unit(g, at, j, 0)
                        if u:
                            n = u[0] * NKV + u[1]
                            need_alone(dve, exp_done, (n - 1) * REP, v_passed)
                            wait_alone(dve, scored, n + 1, v_passed)
                            for h in range(REP):
                                dve.tensor_tensor_reduce(out=masked[:, j % 2, h, :], in0=s_ps[j % 2][:, h * P:(h + 1) * P],
                                                         in1=mask[:, :], scale=1.0, scalar=3e38, op0=ALU.add, op1=ALU.min,
                                                         accum_out=neg_max[:, j % 2, h:h + 1]).then_inc(masked_done, 1)
                        u = unit(g, at, j, 1)
                        if u:
                            n = u[0] * NKV + u[1]
                            dve.wait_ge(exp_done, n * REP + REP)
                            need(dve, normed_done, n - 1)
                            dve.reciprocal(recip[:, u[1] % 2, :], sums[:, u[1] % 2, :]).then_inc(recip_done, 1)
                        u = unit(g, at, j, 3)
                        if u:
                            n = u[0] * NKV + u[1]
                            dve.wait_ge(weighed, n + 1)
                            if u[1] == 0:
                                need(dve, mixed, u[0])
                            for e in range(2):
                                dve.tensor_copy(oT[HD * e:HD * (e + 1), 2 * u[1]:2 * u[1] + 2, :],
                                                o_ps[HD * e:HD * (e + 1), :].rearrange("p (m e c) -> p m e c", e=2, c=P)[:, :, e, :]
                                                ).then_inc(o_ready, 1)
                        if at is None or 0 <= at - 2 < G:
                            n = (g - 2) * NKV + j
                            dve.wait_ge(inverted, n + 1)
                            rows = xres[:, bass.ds(n * 2, 2), :]
                            dve.tensor_tensor(rows, rows, out_ps[j % 2][:, :].rearrange("p (t d) -> p t d", t=2),
                                              ALU.add).then_inc(added, 1)

                all_groups(dve, group)

            @block.tensor
            def _(pe):
                pe.wait_ge(loaded, LOADS)
                pe.wait_ge(const_ready, 3)
                for n, (what, m, at) in enumerate(UNITS):
                    if n >= 8:
                        pe.wait_ge((act_took, dve_took)[n % 2], taken_count(n % 2, n - 7))
                    for k in range(KD):
                        if what == "v":
                            pe_l, pe_r = x_rows(k, at), v_wT[:, k, :, :, :].rearrange("p j e d -> p (j e d)")
                        else:
                            pe_l = (q_wT[:, k, m * P:(m + 1) * P] if what == "q" else
                                    k_wT[:, k, m, :, :].rearrange("p e d -> p (e d)"))
                            pe_r = C.xlow[:, k, at * G:(at + 1) * G, :, :].rearrange("p b r f -> p (b r f)")
                        ins = pe.matmul(ps[n % 8][:, :], pe_l, pe_r, start=(k == 0), stop=(k == KD - 1))
                    ins.then_inc(proj_done, 1)
                pe.wait_ge(act_took, taken_count(0, len(UNITS)))
                pe.wait_ge(dve_took, taken_count(1, len(UNITS)))

                def group(g, at):
                    for j in range(NKV):
                        u = unit(g, at, j, 0)
                        if u:
                            n = u[0] * NKV + u[1]
                            need(pe, masked_done, (n - 1) * REP)
                            for m in range(2):
                                ins = pe.matmul(s_ps[j % 2][:, m * 2 * P:(m + 1) * 2 * P],
                                                qT[:, 2 * j + m, bass.ds(g, 1), :].rearrange("p a c -> p (a c)"),
                                                kT[:, bass.ds(g, 1), j, :, :].rearrange("p a e c -> p (a e c)"), start=True, stop=True)
                            ins.then_inc(scored, 1)
                        u = unit(g, at, j, 2)
                        if u:
                            n = u[0] * NKV + u[1]
                            pe.wait_ge(normed_done, n + 1)
                            need(pe, pt_ready, n - 1)
                            for h in range(REP):
                                ins = pe.transpose(t_ps[u[1] % 2][:, h * P:(h + 1) * P], normed[:, u[1] % 2, h, :], ident[:, :])
                            ins.then_inc(turned, 1)
                        u = unit(g, at, j, 3)
                        if u:
                            n = u[0] * NKV + u[1]
                            pe.wait_ge(pt_ready, n + 1)
                            need(pe, o_ready, n * 2)
                            pe.matmul(o_ps[:, :], v[:, bass.ds(u[0], 1), u[1] * 2 * HD:(u[1] + 1) * 2 * HD]
                                      .rearrange("p a d -> p (a d)"),
                                      probsT[:, u[1] % 2, :, :].rearrange("p h c -> p (h c)"), start=True,
                                      stop=True).then_inc(weighed, 1)
                        if at is None or 0 <= at - 2 < G:
                            n = (g - 2) * NKV + j
                            pe.wait_ge(low_ready, g - 1)
                            need(pe, added, n - 1)
                            for t in range(2):
                                ins = pe.matmul(out_ps[j % 2][:, t * D:(t + 1) * D], idft[:, 2 * j + t, :], low[:, :],
                                                start=True, stop=True)
                            ins.then_inc(inverted, 1)
                    if at is None or 0 <= at - 1 < G:
                        pe.wait_ge(o_ready, g * (2 * NKV))
                        need(pe, low_ready, g - 1)
                        for k in range(KD):
                            for m in range(NQ):
                                ins = pe.matmul(proj_ps[:, k * P:(k + 1) * P], oT[:, m, :], o_wT[:, m, k * P:(k + 1) * P],
                                                start=(m == 0), stop=False)
                            ins = pe.matmul(proj_ps[:, k * P:(k + 1) * P], x_rows(k, g - 1), neg_ident[:, :],
                                            start=False, stop=True)
                        ins.then_inc(mixed, 1)

                all_groups(pe, group)


def position_weights(nc, C, ctx):
    D, S, H = C.D, C.S, C.H
    KD = D // P
    TAIL = S + S // H

    def sb(name, shape):
        return ctx.enter_context(nc.sbuf_tensor(f"b_{name}", shape, F32))

    ext_dram = nc.dram_tensor("b_ext", [TAIL + P - 1, H], F32, kind="Internal").ap()
    C.bias_tab = sb("bias_tab", [P, TAIL * H])
    C.w_in_sb = sb("w_in", [P, KD, 3 * D])
    C.w_out_sb = sb("w_out", [P, KD, D])
    C.b_cols = sb("b_cols", [P, 2, KD])
    C.b_v = sb("b_v", [P, D])
    C.b_o = sb("b_o", [P, D])
    ext_written = ctx.enter_context(nc.semaphore("b_ext_written"))
    C.tab_loaded = ctx.enter_context(nc.semaphore("b_tab_loaded"))
    C.position_loaded = ctx.enter_context(nc.semaphore("b_loaded"))

    def load(sp):
        sp.dma_start(ext_dram[0:S, :], C.rel_emb[S:2 * S, :]).then_inc(ext_written, 16)
        sp.dma_start(ext_dram[S:TAIL + P - 1, :],
                     C.rel_emb[2 * S - 1:2 * S, :].broadcast_to([TAIL + P - 1 - S, H])).then_inc(ext_written, 16)
        done = C.position_loaded
        sp.dma_start(C.w_in_sb[:, :, :], C.w_in.rearrange("(k p) e -> p k e", p=P)).then_inc(done, 16)
        sp.dma_start(C.w_out_sb[:, :, :], C.w_out.rearrange("(k p) e -> p k e", p=P)).then_inc(done, 16)
        sp.dma_start(C.b_cols[:, :, :], C.b_in[0:2 * D].rearrange("(s k p) -> p s k", s=2, p=P),
                     allow_slow_non_contiguous=True).then_inc(done, 16)
        sp.dma_start(C.b_v[:, :], C.b_in[2 * D:3 * D].unsqueeze(0).broadcast_to([P, D])).then_inc(done, 16)
        sp.dma_start(C.b_o[:, :], C.b_out.unsqueeze(0).broadcast_to([P, D])).then_inc(done, 16)
        sp.wait_ge(ext_written, 32)
        sp.dma_start(C.bias_tab[:, :], bass.AP(tensor=ext_dram.tensor, offset=0,
                                               ap=[[H, P], [1, TAIL * H]])).then_inc(C.tab_loaded, 16)

    return load


def position_attention(nc, C):
    D, S, B, H = C.D, C.S, C.B, C.H
    HD = D // H
    KD = D // P
    QT = S // P
    HG = 4
    A = S // H
    UNIT = 8
    STEPS = H * QT
    UNITS = STEPS // UNIT
    xres, ident = C.xres, C.ident
    Q_PARTS = (0, 0, 1, 0, 2, 1)
    K_PARTS = (0, 1, 0, 2, 0, 1)
    COPIES = len(Q_PARTS)

    with ExitStack() as ctx:
        def sb(name, shape, dt=F32):
            return ctx.enter_context(nc.sbuf_tensor(f"b_{name}", shape, dt))

        def sem(name):
            return ctx.enter_context(nc.semaphore(f"b_{name}"))

        s_ps = [ctx.enter_context(nc.psum_tensor(f"b_s_ps{n}", [P, S], F32)) for n in range(2)]
        t_ps = [ctx.enter_context(nc.psum_tensor(f"b_t_ps{n}", [P, QT, P], F32)) for n in range(4)]
        o_ps = ctx.enter_context(nc.psum_tensor("b_o_ps", [P, 2, 2 * P], F32))
        misc = ctx.enter_context(nc.psum_tensor("b_misc", [P, 512], F32))

        parts_dram = [nc.dram_tensor(f"b_{side}_parts", [2, P, 3, S], BF16, kind="Internal").ap() for side in "qk"]

        bias_tab, w_in, w_out, b_cols, b_v, b_o = C.bias_tab, C.w_in_sb, C.w_out_sb, C.b_cols, C.b_v, C.b_o
        tab_loaded, loaded = C.tab_loaded, C.position_loaded
        stacks = [sb(f"{side}_stacks", [P, 2, HG, S], BF16) for side in "qk"]
        probsT = sb("probsT", [P, 2, HG, QT, 2 * P])
        stats = sb("stats", [P, 4, 6])
        mv = sb("mv", [P, 4, 2])
        var_eps = sb("var_eps", [P, 4])
        rstd = sb("rstd", [P, 4])
        mhalf = sb("mhalf", [P, 4])
        zero = sb("zero", [P, 1])
        xn = sb("xn", [P, QT, D])
        xnT = sb("xnT", [P, KD, S])
        v_sb = sb("v_sb", [P, QT, D + HD])
        probs = sb("probs", [P, 8, S])
        neg_max = sb("neg_max", [P, 8])
        sums = sb("sums", [P, 4, 2, HG])
        recip = sb("recip", [P, 2, 2, HG])
        proj = sb("proj", [P, 2, S])
        rest = sb("rest", [P, S])
        parts = sb("parts", [P, 2, 3, S], BF16)
        o_sb = sb("o_sb", [P, 2, 2 * P])
        o_tok = sb("o_tok", [P, QT, D])
        oT = sb("oT", [P, KD, S])

        tab_ready = sem("tab_ready")
        const_ready = sem("const_ready")
        stacks_clear = sem("stacks_clear")
        qb_ready = sem("qb_ready")
        stats_ready = sem("stats_ready")
        mv_ready = sem("mv_ready")
        var_ready = sem("var_ready")
        rstd_ready = sem("rstd_ready")
        xn_ready = sem("xn_ready")
        split_step = sem("split_step")
        written = [sem(f"{side}_written") for side in "qk"]
        stack_in = [sem(f"stack_in{n}") for n in range(2)]
        s_done = sem("s_done")
        biased_done = sem("biased_done")
        exp_done = sem("exp_done")
        turned = sem("turned")
        pt_even = sem("pt_even")
        pt_odd = sem("pt_odd")
        pv_done = sem("pv_done")
        o_taken = sem("o_taken")
        o_turned = sem("o_turned")
        o_scaled = sem("o_scaled")
        recip_done = sem("recip_done")
        misc_done = sem("misc_done")
        misc_free = sem("misc_free")
        preadded = sem("preadded")
        v_passed, p_passed = C.vector_passed, C.pool_passed
        LEAD = 0
        LAG = 3
        READ = 16 * 2 * COPIES

        USES = [(10, "v0"), (13, "v1"), (15, "oT0"), (17, "oT1"), (20, "out0"), (27, "out1"), (29, "xT0"), (32, "xT1"),
                (35, "qk0"), (38, "qk1"), (43, "qk2"), (51, "qk3")]
        OF_LAST_BATCH = ("oT0", "oT1", "out0", "out1")
        OF_NEXT_BATCH = ("xT0", "xT1", "qk0", "qk1", "qk2", "qk3")
        WEIGH, TAKE, TURN = 14, 18, 20
        names = {
            "start": list(OF_NEXT_BATCH),
            "first": [u for _, u in USES if u not in OF_LAST_BATCH],
            "mid": [u for _, u in USES],
            "last": [u for _, u in USES if u not in OF_NEXT_BATCH],
            "end": list(OF_LAST_BATCH),
        }

        def uses_before(b, kind, use):
            ahead, behind = len(OF_NEXT_BATCH), len(OF_LAST_BATCH)
            base = {"start": 0, "first": ahead, "mid": b * len(USES) + (ahead - behind),
                    "last": b * len(USES) + (ahead - behind), "end": b * len(USES) - behind}[kind]
            return base + names[kind].index(use)

        def all_batches(eng, slot):
            for t in range(STEPS):
                slot(0, "first", t)
            with eng.Fori(1, B - 1) as b:
                for t in range(STEPS):
                    slot(b, "mid", t)
            for t in range(STEPS):
                slot(B - 1, "last", t)
            for t in range(32):
                slot(B, "end", t)

        def in_step(kind, t, use, lead=0):
            return use in names[kind] and (t + lead, use) in USES

        def of_unit(kind, t, delay):
            return (t - delay) % UNIT == 0 and not (kind == "first" and t < delay) and not (kind == "end" and t >= delay)

        def evacuate(eng, b, t, ready):
            u, h, ql = t % STEPS // UNIT, t % UNIT // 2, t % 2
            if t % UNIT < 2:
                need(eng, pv_done, b * UNITS + t // UNIT - 1)
            eng.wait_ge(turned, b * STEPS + t + 1)
            dst = probsT[:, u % 2, h, :, ql * P:(ql + 1) * P]
            if ql == 0:
                eng.tensor_copy(dst, t_ps[t % 4][:, :, :]).then_inc(ready, 1)
            else:
                eng.activation(dst, t_ps[t % 4][:, :, :], ACT.Copy).then_inc(ready, 1)

        with nc.Block() as block:
            @block.sync
            def _(sp):
                def write(n, m, side):
                    sp.wait_ge(split_step, 8 * n + 4 * side + 4)
                    sp.dma_start(parts_dram[side][m], parts[:, side, :, :]).then_inc(written[side], 16)

                def read(g, pair):
                    m, slot = g // 2, g % 2
                    for side in range(2):
                        sp.wait_ge(written[side], 16 * pair + 16)
                        for c, part in enumerate((Q_PARTS, K_PARTS)[side]):
                            src = parts_dram[side][m, HG * HD * slot:HG * HD * (slot + 1), part, :]
                            sp.dma_start(stacks[side][HD * c:HD * (c + 1), slot, :, :],
                                         src.rearrange("(h d) q -> d h q", d=HD)).then_inc(stack_in[slot], 16)

                def batch(b, last):
                    sp.wait_ge(s_done, 16 * (b * 4 + 1))
                    read(2, b * 2 + 1)
                    sp.wait_ge(s_done, 16 * (b * 4 + 2))
                    read(3, b * 2 + 1)
                    if not last:
                        for slot in range(2):
                            sp.wait_ge(stack_in[slot], READ * (b * 2 + 1))
                        write(b * 2 + 2, 0, 0)
                        write(b * 2 + 2, 0, 1)
                        sp.wait_ge(s_done, 16 * (b * 4 + 3))
                        read(0, b * 2 + 2)
                        for slot in range(2):
                            sp.wait_ge(stack_in[slot], READ * (b * 2 + 2))
                        write(b * 2 + 3, 1, 0)
                        write(b * 2 + 3, 1, 1)
                        sp.wait_ge(s_done, 16 * (b * 4 + 4))
                        read(1, b * 2 + 2)

                write(0, 0, 0)
                write(0, 0, 1)
                read(0, 0)
                read(1, 0)
                write(1, 1, 0)
                write(1, 1, 1)
                with sp.Fori(0, B - 1) as b:
                    batch(b, False)
                batch(B - 1, True)
                for side in range(2):
                    sp.wait_ge(written[side], 16 * 2 * B)

            @block.gpsimd
            def _(pool):
                pool.memset(mhalf[:, :], -0.5).then_inc(const_ready, 1)
                pool.memset(zero[:, :], 0.0).then_inc(const_ready, 1)
                pool.memset(v_sb[:, :, D:], 0.0).then_inc(const_ready, 1)
                pool.wait_ge(const_ready, 3)
                pool.wait_ge(loaded, 16 * 5)
                pool.tensor_scalar(b_cols[:, 0, :], b_cols[:, 0, :], -HD ** -0.5, None, ALU.mult).then_inc(qb_ready, 1)

                def rstd_of(b):
                    wait_alone(pool, mv_ready, b * 4 + 4, p_passed)
                    pool.tensor_scalar(var_eps[:, :], mv[:, :, 1], EPS, None, ALU.add).then_inc(var_ready, 1)
                    pool.wait_ge(var_ready, b + 1)
                    pool.tensor_tensor(rstd[:, :], var_eps[:, :], mhalf[:, :], ALU.pow).then_inc(rstd_ready, 1)

                def split(b, kind, i):
                    nb = b if kind == "start" else b + 1
                    n, side = nb * 4 + i, i % 2
                    pool.wait_ge(misc_free, uses_before(b, kind, f"qk{i}") + 1)
                    need(pool, written[side], 16 * (nb * 2 + i // 2))
                    src, at = proj[:, side, :], n * 4
                    pool.tensor_tensor(parts[:, side, 0, :], src, zero[:, 0:1].broadcast_to([P, S]),
                                       ALU.add).then_inc(split_step, 1)
                    pool.wait_ge(split_step, at + 1)
                    pool.tensor_tensor(rest[:, :], src, parts[:, side, 0, :], ALU.subtract).then_inc(split_step, 1)
                    pool.wait_ge(split_step, at + 2)
                    pool.tensor_tensor(parts[:, side, 1, :], rest[:, :], zero[:, 0:1].broadcast_to([P, S]),
                                       ALU.add).then_inc(split_step, 1)
                    pool.wait_ge(split_step, at + 3)
                    pool.tensor_tensor(parts[:, side, 2, :], rest[:, :], parts[:, side, 1, :],
                                       ALU.subtract).then_inc(split_step, 1)

                def batch(b, kind):
                    pool.wait_ge(xn_ready, b * 4 + 4)
                    pool.tensor_tensor(xres[:, bass.ds(b * QT, QT), :], xres[:, bass.ds(b * QT, QT), :],
                                       b_o[:, :].unsqueeze(1).broadcast_to([P, QT, D]), ALU.add).then_inc(preadded, 1)
                    if kind != "last":
                        rstd_of(b + 1)
                        for i in range(4):
                            split(b, kind, i)

                rstd_of(0)
                pool.wait_ge(rstd_ready, 1)
                for side in range(2):
                    if side:
                        pool.wait_ge(stacks_clear, side)
                    pool.memset(stacks[side][HD * COPIES:, :, :, :].rearrange("p a h q -> p (a h q)"), 0.0
                                ).then_inc(stacks_clear, 1)
                pool.wait_ge(stacks_clear, 2)
                for i in range(4):
                    split(0, "start", i)
                batch(0, "first")
                with pool.Fori(1, B - 1) as b:
                    batch(b, "mid")
                batch(B - 1, "last")

            @block.scalar
            def _(act):
                def take_xT(b, kind, k):
                    act.wait_ge(misc_done, uses_before(b, kind, f"xT{k}") + 1)
                    act.activation(xnT[:, k, :], misc[:, :], ACT.Copy).then_inc(misc_free, 1)

                def take_qk(b, kind, i):
                    nb = b if kind == "start" else b + 1
                    side, m = i % 2, i // 2
                    act.wait_ge(misc_done, uses_before(b, kind, f"qk{i}") + 1)
                    need(act, split_step, 4 * (nb * 4 + i - 1))
                    if side == 0:
                        act.activation(proj[:, 0, :].rearrange("p (b a) -> p a b", a=A)[:, ::-1, :],
                                       misc[:, :].rearrange("p (a b) -> p a b", a=A), ACT.Identity,
                                       bias=b_cols[:, 0, m:m + 1], scale=-HD ** -0.5).then_inc(misc_free, 1)
                    else:
                        act.activation(proj[:, 1, :], misc[:, :], ACT.Identity,
                                       bias=b_cols[:, 1, m:m + 1]).then_inc(misc_free, 1)

                def slot(b, kind, t):
                    if (t - LAG) % 2 == 0 and not (kind == "first" and t < LAG + 2) and not (kind == "end" and t > LAG):
                        evacuate(act, b, t - (LAG + 1), pt_odd)
                    if kind != "end":
                        u, T = t // UNIT, b * STEPS + t
                        h, ql = t % UNIT // 2, t % 2
                        act.wait_ge(biased_done, T + 1)
                        if t % UNIT == 0:
                            need(act, recip_done, b * UNITS + u - 3)
                        act.activation(probs[:, t % 8, :], probs[:, t % 8, :], ACT.Exp, bias=neg_max[:, t % 8:t % 8 + 1],
                                       scale=-1.0, accum_out=sums[:, u % 4, ql, h:h + 1]).then_inc(exp_done, 1)
                    if of_unit(kind, t, TAKE):
                        u = (t - TAKE) % STEPS // UNIT
                        n = b * UNITS + (t - TAKE) // UNIT
                        act.wait_ge(pv_done, n + 1)
                        need(act, recip_done, n - 1)
                        act.activation(o_sb[:, u % 2, :], o_ps[:, u % 2, :], ACT.Copy).then_inc(o_taken, 1)
                    for k in range(2):
                        if in_step(kind, t, f"xT{k}", LEAD):
                            take_xT(b, kind, k)
                        if in_step(kind, t, f"oT{k}", LEAD):
                            act.wait_ge(misc_done, uses_before(b, kind, f"oT{k}") + 1)
                            act.activation(oT[:, k, :].rearrange("p (a b) -> p b a", a=A)[:, :, ::-1],
                                           misc[:, :].rearrange("p (b a) -> p b a", a=A), ACT.Copy).then_inc(misc_free, 1)
                    for i in range(4):
                        if in_step(kind, t, f"qk{i}", LEAD):
                            take_qk(b, kind, i)

                act.wait_ge(qb_ready, 1)
                take_xT(0, "start", 0)
                take_xT(0, "start", 1)
                for i in range(4):
                    take_qk(0, "start", i)
                all_batches(act, slot)

            @block.vector
            def _(dve):
                def stats_of(b, j):
                    dve.bn_stats(stats[:, j, :], xres[:, bass.ds(b * QT + j, 1), :].rearrange("p a d -> p (a d)")
                                 ).then_inc(stats_ready, 1)

                def mean_var_of(b):
                    wait_alone(dve, stats_ready, b * QT + QT, v_passed)
                    for j in range(QT):
                        dve.bn_aggr(mv[:, j, :], stats[:, j, :]).then_inc(mv_ready, 1)

                def norm(b, j):
                    if j == 0:
                        dve.wait_ge(rstd_ready, b + 1)
                    dve.tensor_scalar(xn[:, j, :], xres[:, bass.ds(b * QT + j, 1), :].rearrange("p a d -> p (a d)"),
                                      mv[:, j, 0:1], rstd[:, j:j + 1], ALU.subtract, ALU.mult).then_inc(xn_ready, 1)

                def slot(b, kind, t):
                    T = b * STEPS + t
                    if (t - LAG) % 2 and not (kind == "first" and t < LAG + 1) and not (kind == "end" and t > LAG):
                        evacuate(dve, b, t - (LAG + 1), pt_even)
                    if kind != "end":
                        h, qt = t // 16 * HG + t % UNIT // 2, t // UNIT % 2 * 2 + t % 2
                        window = min(P // A * qt - h, 1) + H - 1
                        need_alone(dve, turned, T - 7, v_passed)
                        wait_alone(dve, s_done, T + 1, v_passed)
                        dve.tensor_tensor_reduce(out=probs[:, t % 8, :], in0=s_ps[t % 2][:, :],
                                                 in1=bias_tab[:, window * S:(window + 1) * S], scale=1.0, scalar=3e38,
                                                 op0=ALU.add, op1=ALU.min,
                                                 accum_out=neg_max[:, t % 8:t % 8 + 1]).then_inc(biased_done, 1)
                    if of_unit(kind, t, TURN):
                        u = (t - TURN) % STEPS // UNIT
                        n = b * UNITS + (t - TURN) // UNIT
                        g, qp = u // 2, u % 2
                        dve.wait_ge(o_turned, n + 1)
                        dve.reciprocal(recip[:, u % 2, :, :], sums[:, u % 4, :, :]).then_inc(recip_done, 1)
                        if u == 0 and kind in ("mid", "last"):
                            dve.wait_ge(misc_done, uses_before(b, kind, "oT1") + 1)
                        dve.wait_ge(recip_done, n + 1)
                        dve.tensor_tensor(
                            o_tok[:, 2 * qp:2 * qp + 2, g * HG * HD:(g + 1) * HG * HD].rearrange("p q (h d) -> p q h d", h=HG),
                            o_ps[:, u % 2, :].rearrange("p (q h d) -> p q h d", q=2, h=HG)[:, :, :, 0:HD],
                            recip[:, u % 2, :, :].unsqueeze(3).broadcast_to([P, 2, HG, HD]),
                            ALU.mult).then_inc(o_scaled, 1)
                    for j in range(2):
                        if in_step(kind, t, f"v{j}", LEAD):
                            dve.wait_ge(misc_done, uses_before(b, kind, f"v{j}") + 1)
                            dve.tensor_tensor(v_sb[:, 2 * j:2 * j + 2, 0:D], misc[:, :].rearrange("p (t d) -> p t d", t=2),
                                              b_v[:, :].unsqueeze(1).broadcast_to([P, 2, D]), ALU.add).then_inc(misc_free, 1)
                        if in_step(kind, t, f"out{j}", LEAD):
                            rows = xres[:, bass.ds((b - 1) * QT + 2 * j, 2), :]
                            if j == 0:
                                dve.wait_ge(preadded, b)
                            dve.wait_ge(misc_done, uses_before(b, kind, f"out{j}") + 1)
                            dve.tensor_tensor(rows, rows, misc[:, :].rearrange("p (t d) -> p t d", t=2),
                                              ALU.add).then_inc(misc_free, 1)
                    if kind in ("first", "mid"):
                        if 1 <= t < 1 + QT:
                            stats_of(b + 1, t - 1)
                        if t == 1 + QT:
                            mean_var_of(b + 1)
                        if 22 <= t < 22 + QT:
                            norm(b + 1, t - 22)

                for j in range(QT):
                    stats_of(0, j)
                mean_var_of(0)
                for j in range(QT):
                    norm(0, j)
                dve.wait_ge(tab_loaded, 16)
                dve.tensor_scalar(bias_tab[:, :], bias_tab[:, :], -1.0, None, ALU.mult).then_inc(tab_ready, 1)
                dve.wait_ge(tab_ready, 1)
                dve.wait_ge(loaded, 16 * 5)
                all_batches(dve, slot)

            @block.tensor
            def _(pe):
                def bank(b, kind, use):
                    need(pe, misc_free, uses_before(b, kind, use))

                def turn_x(b, kind, k):
                    nb = b if kind == "start" else b + 1
                    pe.wait_ge(xn_ready, nb * QT + QT)
                    bank(b, kind, f"xT{k}")
                    for j in range(QT):
                        ins = pe.transpose(misc[:, j * P:(j + 1) * P], xn[:, j, k * P:(k + 1) * P], ident[:, :])
                    ins.then_inc(misc_done, 1)

                def project_qk(b, kind, i, k):
                    if k == 0:
                        bank(b, kind, f"qk{i}")
                    at = (i % 2) * D + (i // 2) * P
                    ins = pe.matmul(misc[:, :], w_in[:, k, at:at + P], xnT[:, k, :], start=(k == 0), stop=(k == KD - 1))
                    if k == KD - 1:
                        ins.then_inc(misc_done, 1)

                def project_rows(b, kind, use, j, i, rowsT, w):
                    if i == 0:
                        bank(b, kind, use)
                    for k in range(KD):
                        ins = pe.matmul(misc[:, i * D:(i + 1) * D], rowsT[:, k, (2 * j + i) * P:(2 * j + i + 1) * P],
                                        w[:, k, :], start=(k == 0), stop=(k == KD - 1))
                    if i == 1:
                        ins.then_inc(misc_done, 1)

                def weigh(b, kind, u, n, kt):
                    g = u // 2
                    if kt == 0:
                        pe.wait_ge(pt_even, 4 * n + 4)
                        pe.wait_ge(pt_odd, 4 * n + 4)
                        need(pe, o_scaled, n)
                    if u == 0 and kt % 2 == 0:
                        pe.wait_ge(misc_free, uses_before(b, kind, f"v{kt // 2}") + 1)
                    for h in range(HG):
                        head = g * HG + h
                        ins = pe.matmul(o_ps[32 * h:32 * (h + 1), u % 2, :], v_sb[:, kt, head * HD:head * HD + 32],
                                        probsT[:, u % 2, h, kt, :], start=(kt == 0), stop=(kt == QT - 1),
                                        tile_position=(0, 32 * h))
                    if kt == QT - 1:
                        ins.then_inc(pv_done, 1)

                def slot(b, kind, t):
                    T = b * STEPS + t
                    if kind != "end":
                        g = t // 16
                        h, qt = t % UNIT // 2, t // UNIT % 2 * 2 + t % 2
                        if t % 16 == 0:
                            pe.wait_ge(stack_in[g % 2], READ * (b * 2 + g // 2 + 1))
                        need(pe, biased_done, T - 1)
                        pe.matmul(s_ps[t % 2][:, :], stacks[0][:, g % 2, h, qt * P:(qt + 1) * P], stacks[1][:, g % 2, h, :],
                                  start=True, stop=True).then_inc(s_done, 1)
                    td = (t - LAG) % STEPS
                    if not (kind == "first" and t < LAG) and not (kind == "end" and t > LAG - 1):
                        pe.wait_ge(exp_done, T - (LAG - 1))
                        need(pe, (pt_even, pt_odd)[td % 2], b * (STEPS // 2) + (t - LAG - td % 2) // 2 - 1)
                        for kt in range(QT):
                            ins = pe.transpose(t_ps[td % 4][:, kt, :], probs[:, td % 8, kt * P:(kt + 1) * P], ident[:, :])
                        ins.then_inc(turned, 1)
                    for kt in range(QT):
                        if of_unit(kind, t, WEIGH + kt):
                            weigh(b, kind, (t - WEIGH - kt) % STEPS // UNIT, b * UNITS + (t - WEIGH - kt) // UNIT, kt)
                    if of_unit(kind, t, TURN):
                        u = (t - TURN) % STEPS // UNIT
                        pe.wait_ge(o_taken, b * UNITS + (t - TURN) // UNIT + 1)
                        for i in range(2):
                            ins = pe.transpose(o_ps[:, u % 2, i * P:(i + 1) * P], o_sb[:, u % 2, i * P:(i + 1) * P], ident[:, :])
                        ins.then_inc(o_turned, 1)
                    for j in range(2):
                        for i in range(2):
                            if in_step(kind, t, f"v{j}", 1 - i):
                                project_rows(b, kind, f"v{j}", j, i, xnT, w_in[:, :, 2 * D:3 * D])
                            if in_step(kind, t, f"out{j}", 1 - i):
                                project_rows(b, kind, f"out{j}", j, i, oT, w_out)
                        if in_step(kind, t, f"xT{j}"):
                            turn_x(b, kind, j)
                        if in_step(kind, t, f"oT{j}"):
                            bank(b, kind, f"oT{j}")
                            pe.wait_ge(o_scaled, b * UNITS)
                            for qt in range(QT):
                                ins = pe.transpose(misc[:, qt * P:(qt + 1) * P], o_tok[:, qt, j * P:(j + 1) * P], ident[:, :])
                            ins.then_inc(misc_done, 1)
                    for i in range(4):
                        for k in range(KD):
                            if in_step(kind, t, f"qk{i}", 1 - k):
                                project_qk(b, kind, i, k)

                pe.wait_ge(loaded, 16 * 5)
                pe.wait_ge(const_ready, 3)
                pe.wait_ge(stacks_clear, 2)
                turn_x(0, "start", 0)
                turn_x(0, "start", 1)
                for i in range(4):
                    for k in range(KD):
                        project_qk(0, "start", i, k)
                all_batches(pe, slot)


def token_ffn(nc, C, which, out_dram, load_ahead=None):
    NT, D, E, TG = C.NT, C.D, C.E, C.TG
    KD = D // P
    NG = NT // TG
    xres, ident = C.xres, C.ident

    with ExitStack() as ctx:
        def sb(name, shape, dt=F32):
            return ctx.enter_context(nc.sbuf_tensor(f"{name}{which}", shape, dt))

        def sem(name):
            return ctx.enter_context(nc.semaphore(f"{name}{which}"))

        main = [ctx.enter_context(nc.psum_tensor(f"experts{n}_{which}", [P, 512], F32)) for n in range(4)]
        xT_ps = [ctx.enter_context(nc.psum_tensor(f"xT_ps{n}_{which}", [P, 512], F32)) for n in range(2)]
        small_ps = ctx.enter_context(nc.psum_tensor(f"small_ps_{which}", [P, 512], F32))
        bias_ps = ctx.enter_context(nc.psum_tensor(f"bias_ps_{which}", [P, 512], F32))
        logit_ps = small_ps[:, 0:TG * E].rearrange("p (t e) -> p t e", t=TG)
        gT_ps = small_ps[:, 128:256]

        w32 = sb("w32", [P, KD, E, D])
        w_hi = sb("w_hi", [P, KD, E * D], F16)
        w_lo = sb("w_lo", [P, KD, E * D], F16)
        gw32 = sb("gw32", [P, KD, E])
        gw_hi = sb("gw_hi", [P, KD, E], F16)
        gw_lo = sb("gw_lo", [P, KD, E], F16)
        gate_b = sb("gate_b", [P, TG, E])
        eb_rows = sb("eb_rows", [P, TG, D])
        wmax = sb("wmax", [P, 2])
        wmax_all = sb("wmax_all", [P, 2])
        scale = sb("scale", [P, 2])
        unscale = sb("unscale", [P, 2])
        iota8 = sb("iota8", [P, TG, E])
        stats = sb("stats", [P, TG, 6])
        mv = sb("mv", [P, TG, 2])
        var_eps = sb("var_eps", [P, TG])
        rstd = sb("rstd", [P, TG])
        mhalf = sb("mhalf", [P, TG])
        xn = sb("xn", [P, TG, D])
        xT_hi = sb("xT_hi", [P, 2, TG, KD, P], F16)
        xT_lo = sb("xT_lo", [P, 2, TG, KD, P], F16)
        logits = sb("logits", [P, TG, E])
        top = sb("top", [P, TG, 8])
        top_at = sb("top_at", [P, TG, 8], U32)
        is_top = sb("is_top", [P, 2, TG, E])
        kept = sb("kept", [P, TG, E])
        below = sb("below", [P, TG, E])
        expd = sb("expd", [P, TG, E])
        gz = sb("gz", [P, TG, E])
        gsum = sb("gsum", [P, TG])
        grec = sb("grec", [P, TG])
        gates = sb("gates", [P, P])
        gscaled = sb("gscaled", [P, 2, TG, E])
        gT = sb("gT", [P, P])
        acc = sb("acc", [P, TG, D])
        part = sb("part", [P, 2, 4, D])
        pair = sb("pair", [P, 2, 2, D])
        rest = sb("rest", [P, 2, D])

        w_loaded = sem("w_loaded")
        zeroed = sem("zeroed")
        const_ready = sem("const_ready")
        wmax_ready = sem("wmax_ready")
        wmax_all_ready = sem("wmax_all_ready")
        prep_step = sem("prep_step")
        w_ready = sem("w_ready")
        w_hi_ready = sem("w_hi_ready")
        stats_ready = sem("stats_ready")
        mv_ready = sem("mv_ready")
        var_ready = sem("var_ready")
        rstd_ready = sem("rstd_ready")
        xn_ready = sem("xn_ready")
        xT_done = sem("xT_done")
        hi_ready = sem("hi_ready")
        lo_ready = sem("lo_ready")
        logits_done = sem("logits_done")
        gate_step = sem("gate_step")
        below_ready = sem("below_ready")
        gate_mass = sem("gate_mass")
        rec_ready = sem("rec_ready")
        exp_ready = sem("exp_ready")
        gates_ready = sem("gates_ready")
        gT_done = sem("gT_done")
        gT_ready = sem("gT_ready")
        bank_done = sem("bank_done")
        vector_free = sem("vector_free")
        scalar_free = sem("scalar_free")
        bias_done = sem("bias_done")
        acc_step = sem("acc_step")
        pair_ready = sem("pair_ready")
        rest_ready = sem("rest_ready")
        tile_done = sem("tile_done")
        stored = sem("stored")
        vector_passed, pool_passed = C.vector_passed, C.pool_passed

        ORDER = (0, 2, 1, 3)

        def pipelined(eng, group):
            with eng.Fori(0, NG // 2 - 1) as i:
                group(i * 2, 0, 2)
                group(i * 2 + 1, 1, 2)
            group(NG - 2, 0, 1)
            group(NG - 1, 1, 0)

        with nc.Block() as block:
            @block.sync
            def _(sp):
                sp.dma_start(w32[:, :, :, :], C.expert_w.rearrange("(k p) e o -> p k e o", p=P)).then_inc(w_loaded, 16)
                sp.dma_start(gw32[:, :, :], C.gate_wT.rearrange("(k p) e -> p k e", p=P)).then_inc(w_loaded, 16)
                sp.dma_start(gate_b[:, :, :], C.gate_b.rearrange("(a b e) -> a b e", a=1, b=1)
                             .broadcast_to([P, TG, E])).then_inc(w_loaded, 16)
                sp.wait_ge(zeroed, 1)
                for j in range(TG):
                    sp.dma_start(eb_rows[E * j:E * (j + 1), j, :], C.expert_b).then_inc(w_loaded, 16)
                if load_ahead is not None:
                    load_ahead(sp)
                if out_dram is not None:
                    with sp.Fori(0, NG) as g:
                        sp.wait_ge(tile_done, g * TG + TG + 4)
                        sp.dma_start(out_dram[:, bass.ds(g * TG, TG), :],
                                     xres[:, bass.ds(g * TG, TG), :]).then_inc(stored, 16)
                    sp.wait_ge(stored, 16 * NG)

            @block.gpsimd
            def _(pool):
                pool.memset(eb_rows[:, :, :], 0.0).then_inc(zeroed, 1)
                pool.memset(gates[:, :], 0.0).then_inc(const_ready, 1)
                pool.memset(mhalf[:, :], -0.5).then_inc(const_ready, 1)
                pool.iota(iota8[:, :, :], pattern=[[0, TG], [1, E]], base=0, channel_multiplier=0,
                          allow_small_or_imprecise_dtypes=True).then_inc(const_ready, 1)
                def rstd_of(G):
                    wait_alone(pool, mv_ready, G * TG + TG, pool_passed)
                    pool.tensor_scalar(var_eps[:, :], mv[:, :, 1], EPS, LN_SCALE ** -2, ALU.add,
                                       ALU.mult).then_inc(var_ready, 1)
                    pool.wait_ge(var_ready, G + 1)
                    pool.tensor_tensor(rstd[:, :], var_eps[:, :], mhalf[:, :], ALU.pow).then_inc(rstd_ready, 1)

                def sum_parts(G, j):
                    b = j % 2
                    T = G * TG + j
                    pool.wait_ge(scalar_free, T * 4 + 8)
                    pool.tensor_tensor(pair[:, b, :, :], part[:, b, 0:2, :], part[:, b, 2:4, :], ALU.add).then_inc(pair_ready, 1)
                    pool.wait_ge(tile_done, T + 3)
                    pool.wait_ge(pair_ready, T + 1)
                    pool.tensor_tensor(rest[:, b, :], pair[:, b, 0, :], pair[:, b, 1, :], ALU.add).then_inc(rest_ready, 1)

                pool.wait_ge(const_ready, 3)
                rstd_of(0)
                pool.wait_ge(wmax_ready, 2)
                pool.partition_all_reduce(wmax_all[:, :], wmax[:, :], P, RMAX).then_inc(wmax_all_ready, 1)
                rstd_of(1)

                def group(G, par, left):
                    for j in range(TG):
                        if j == 2 and left == 2:
                            rstd_of(G + 2)
                        sum_parts(G, j)

                pipelined(pool, group)

            @block.scalar
            def _(act):
                def split_hi(G, par):
                    for h in range(2):
                        act.wait_ge(xT_done, G * 2 + h + 1)
                        act.activation(xT_hi[:, par, 2 * h:2 * h + 2, :, :],
                                       xT_ps[h][:, :].rearrange("p (t k c) -> p t k c", t=2, k=KD),
                                       ACT.Copy).then_inc(hi_ready, 1)

                def exp_gates(G):
                    act.wait_ge(below_ready, G + 1)
                    act.activation(expd[:, :, :], below[:, :, :], ACT.Exp).then_inc(exp_ready, 1)

                def take_gT(G):
                    act.wait_ge(gT_done, G + 1)
                    act.activation(gT[:, :], gT_ps, ACT.Copy).then_inc(gT_ready, 1)

                def gated_parts(G, par, j):
                    T = G * TG + j
                    for n in (2, 3):
                        act.wait_ge(bank_done, T * 4 + ORDER.index(n) + 1)
                        if n == 2:
                            act.wait_ge(gates_ready, G * 2 + 2)
                            act.wait_ge(rest_ready, T + 1)
                        for h in range(2):
                            e = 2 * n + h
                            act.activation(part[:, j % 2, e - 4, :], main[n][:, h * D:(h + 1) * D], ACT.Copy,
                                           scale=gscaled[:, par, j, e:e + 1]).then_inc(scalar_free, 1)

                act.sem_inc(rest_ready, 2)
                act.sem_inc(scalar_free, 4)
                split_hi(0, 0)
                act.wait_ge(prep_step, 4)
                for n in ORDER:
                    act.activation(w_hi[:, :, n * 512:(n + 1) * 512],
                                   w32[:, :, 2 * n:2 * n + 2, :].rearrange("p k e o -> p k (e o)"), ACT.Copy,
                                   scale=scale[:, 0:1]).then_inc(w_hi_ready, 1)
                exp_gates(0)

                def group(G, par, left):
                    take_gT(G)
                    gated_parts(G, par, 0)
                    if left:
                        split_hi(G + 1, 1 - par)
                    gated_parts(G, par, 1)
                    if left:
                        exp_gates(G + 1)
                    gated_parts(G, par, 2)
                    gated_parts(G, par, 3)

                pipelined(act, group)

            @block.vector
            def _(dve):
                dve.sem_inc(vector_free, 4)
                dve.sem_inc(acc_step, 1)
                dve.sem_inc(tile_done, 4)
                dve.wait_ge(const_ready, 3)

                def row_stats(G):
                    for j in range(TG):
                        dve.bn_stats(stats[:, j, :], xres[:, bass.ds(G * TG + j, 1), :].rearrange("p a d -> p (a d)")
                                     ).then_inc(stats_ready, 1)
                    wait_alone(dve, stats_ready, G * TG + TG, vector_passed)
                    for j in range(TG):
                        dve.bn_aggr(mv[:, j, :], stats[:, j, :]).then_inc(mv_ready, 1)

                def layernorm(G):
                    dve.wait_ge(rstd_ready, G + 1)
                    for j in range(TG):
                        dve.tensor_scalar(xn[:, j, :], xres[:, bass.ds(G * TG + j, 1), :].rearrange("p a d -> p (a d)"),
                                          mv[:, j, 0:1], rstd[:, j:j + 1], ALU.subtract, ALU.mult).then_inc(xn_ready, 1)

                def split_lo(G, par):
                    for h in range(2):
                        dve.wait_ge(hi_ready, G * 2 + h + 1)
                        dve.tensor_tensor(xT_lo[:, par, 2 * h:2 * h + 2, :, :],
                                          xT_ps[h][:, :].rearrange("p (t k c) -> p t k c", t=2, k=KD),
                                          xT_hi[:, par, 2 * h:2 * h + 2, :, :], ALU.subtract).then_inc(lo_ready, 1)

                GS = 2 * TG + 3

                def gates_before_exp(G):
                    dve.wait_ge(logits_done, G + 1)
                    dve.scalar_tensor_tensor(logits[:, :, :], logit_ps, unscale[:, 1:2], gate_b[:, :, :], ALU.mult,
                                             ALU.add).then_inc(gate_step, 1)
                    wait_alone(dve, gate_step, G * GS + 1, vector_passed)
                    for j in range(TG):
                        dve.max(top[:, j, :], logits[:, j, :]).then_inc(gate_step, 1)
                    dve.wait_ge(gate_step, G * GS + 1 + TG)
                    dve.tensor_tensor(below[:, :, :], logits[:, :, :], top[:, :, 0:1].broadcast_to([P, TG, E]),
                                      ALU.subtract).then_inc(below_ready, 1)
                    for j in range(TG):
                        dve.max_index(top_at[:, j, :], top[:, j, :], logits[:, j, :]).then_inc(gate_step, 1)
                    dve.wait_ge(gate_step, G * GS + 1 + 2 * TG)
                    for m in range(2):
                        dve.tensor_tensor(is_top[:, m, :, :], iota8[:, :, :],
                                          top_at[:, :, m:m + 1].broadcast_to([P, TG, E]), ALU.is_equal).then_inc(gate_step, 1)

                def gates_after_exp(G, par):
                    dve.wait_ge(gate_step, G * GS + GS)
                    dve.tensor_tensor(kept[:, :, :], is_top[:, 0, :, :], is_top[:, 1, :, :], ALU.add).then_inc(gate_mass, 1)
                    dve.wait_ge(gate_mass, G * 3 + 1)
                    dve.wait_ge(exp_ready, G + 1)
                    dve.tensor_tensor(gz[:, :, :], expd[:, :, :], kept[:, :, :], ALU.mult).then_inc(gate_mass, 1)
                    dve.wait_ge(gate_mass, G * 3 + 2)
                    dve.tensor_reduce(gsum[:, :], gz[:, :, :], AX.X, ALU.add).then_inc(gate_mass, 1)
                    dve.wait_ge(gate_mass, G * 3 + 3)
                    dve.reciprocal(grec[:, :], gsum[:, :]).then_inc(rec_ready, 1)
                    dve.wait_ge(rec_ready, G + 1)
                    gv = gates[:, 0:TG * E].rearrange("p (t e) -> p t e", t=TG)
                    dve.tensor_tensor(gv, gz[:, :, :], grec[:, :].unsqueeze(2).broadcast_to([P, TG, E]),
                                      ALU.mult).then_inc(gates_ready, 1)
                    dve.wait_ge(gates_ready, G * 2 + 1)
                    dve.tensor_scalar(gscaled[:, par, :, :], gv, unscale[:, 0:1], None, ALU.mult).then_inc(gates_ready, 1)

                def combine(G, par, j):
                    T = G * TG + j
                    x_tile = xres[:, bass.ds(T, 1), :].rearrange("p a d -> p (a d)")
                    if j == 0:
                        dve.wait_ge(gates_ready, G * 2 + 2)
                    dve.wait_ge(tile_done, T + 1)
                    for e in range(4):
                        n, h = e // 2, e % 2
                        if h == 0:
                            dve.wait_ge(bank_done, T * 4 + ORDER.index(n) + 1)
                        if e:
                            dve.wait_ge(vector_free, T * 4 + e + 4)
                        dve.scalar_tensor_tensor(acc[:, j, :], main[n][:, h * D:(h + 1) * D],
                                                 gscaled[:, par, j, e:e + 1], acc[:, j, :] if e else x_tile,
                                                 ALU.mult, ALU.add).then_inc(vector_free, 1)
                    dve.wait_ge(bias_done, T + 1)
                    dve.wait_ge(vector_free, T * 4 + 8)
                    dve.tensor_tensor(acc[:, j, :], acc[:, j, :], bias_ps[:, 0:D], ALU.add).then_inc(acc_step, 1)

                def finish(G, j):
                    T = G * TG + j
                    b = j % 2
                    x_tile = xres[:, bass.ds(T, 1), :].rearrange("p a d -> p (a d)")
                    dve.wait_ge(acc_step, T + 2)
                    dve.wait_ge(rest_ready, T + 3)
                    dve.tensor_tensor(x_tile, acc[:, j, :], rest[:, b, :], ALU.add).then_inc(tile_done, 1)

                row_stats(0)
                layernorm(0)
                dve.wait_ge(w_loaded, 16 * (3 + TG))
                dve.tensor_reduce(wmax[:, 0:1], w32[:, :, :, :], AX.XYZ, ALU.max,
                                  apply_absolute_value=True).then_inc(wmax_ready, 1)
                dve.tensor_reduce(wmax[:, 1:2], gw32[:, :, :], AX.XY, ALU.max,
                                  apply_absolute_value=True).then_inc(wmax_ready, 1)
                dve.wait_ge(wmax_all_ready, 1)
                dve.tensor_scalar(wmax_all[:, :], wmax_all[:, :], 1e-30, 1e30, ALU.max, ALU.min).then_inc(prep_step, 1)
                dve.wait_ge(prep_step, 1)
                dve.reciprocal(scale[:, :], wmax_all[:, :]).then_inc(prep_step, 1)
                dve.wait_ge(prep_step, 2)
                dve.tensor_scalar(scale[:, :].bitcast(I32), scale[:, :].bitcast(I32), 0x7F800000, None,
                                  ALU.bitwise_and).then_inc(prep_step, 1)
                dve.wait_ge(prep_step, 3)
                dve.tensor_scalar(scale[:, :], scale[:, :], W_TOP, None, ALU.mult).then_inc(prep_step, 1)
                dve.wait_ge(prep_step, 4)
                dve.reciprocal(unscale[:, :], scale[:, :]).then_inc(prep_step, 1)
                dve.wait_ge(prep_step, 5)
                dve.tensor_scalar(unscale[:, :], unscale[:, :], 1.0 / LN_SCALE, None, ALU.mult).then_inc(prep_step, 1)
                dve.tensor_scalar(gw_hi[:, :, :], gw32[:, :, :], scale[:, 1:2], None, ALU.mult).then_inc(prep_step, 1)
                dve.wait_ge(prep_step, 7)
                dve.scalar_tensor_tensor(gw_lo[:, :, :], gw32[:, :, :], scale[:, 1:2], gw_hi[:, :, :], ALU.mult,
                                         ALU.subtract).then_inc(w_ready, 1)
                split_lo(0, 0)

                def weights_lo(at):
                    n = ORDER[at]
                    dve.wait_ge(w_hi_ready, at + 1)
                    dve.scalar_tensor_tensor(w_lo[:, :, n * 512:(n + 1) * 512],
                                             w32[:, :, 2 * n:2 * n + 2, :].rearrange("p k e o -> p k (e o)"), scale[:, 0:1],
                                             w_hi[:, :, n * 512:(n + 1) * 512], ALU.mult, ALU.subtract).then_inc(w_ready, 1)

                weights_lo(0)
                gates_before_exp(0)
                weights_lo(1)
                gates_after_exp(0, 0)
                weights_lo(2)
                weights_lo(3)
                row_stats(1)
                layernorm(1)

                def group(G, par, left):
                    combine(G, par, 0)
                    if left:
                        split_lo(G + 1, 1 - par)
                    combine(G, par, 1)
                    finish(G, 0)
                    if left == 2:
                        row_stats(G + 2)
                    if left:
                        gates_before_exp(G + 1)
                    combine(G, par, 2)
                    finish(G, 1)
                    if left:
                        gates_after_exp(G + 1, 1 - par)
                    combine(G, par, 3)
                    finish(G, 2)
                    if left == 2:
                        layernorm(G + 2)
                    finish(G, 3)

                pipelined(dve, group)

            @block.tensor
            def _(pe):
                def turn(G):
                    for j in range(TG):
                        pe.wait_ge(xn_ready, G * TG + j + 1)
                        for k in range(KD):
                            at = (j % 2) * KD * P + k * P
                            ins = pe.transpose(xT_ps[j // 2][:, at:at + P], xn[:, j, k * P:(k + 1) * P], ident[:, :])
                        if j % 2:
                            ins.then_inc(xT_done, 1)

                def gate_logits(G, par):
                    for j in range(TG):
                        if j % 2 == 0:
                            pe.wait_ge(lo_ready, G * 2 + j // 2 + 1)
                        n = 0
                        for k in range(KD):
                            for xs, ws in ((xT_hi, gw_hi), (xT_hi, gw_lo), (xT_lo, gw_hi)):
                                ins = pe.matmul(logit_ps[:, j, :], xs[:, par, j, k, :], ws[:, k, :],
                                                start=(n == 0), stop=(n == 3 * KD - 1))
                                n += 1
                    ins.then_inc(logits_done, 1)

                def turn_gates(G):
                    pe.wait_ge(gates_ready, G * 2 + 1)
                    pe.transpose(gT_ps, gates[:, :], ident[:, :]).then_inc(gT_done, 1)

                def experts(G, par, j):
                    T = G * TG + j
                    for at, n in enumerate(ORDER):
                        if j == 0:
                            pe.wait_ge(w_ready, 2 + at)
                        if n < 2:
                            pe.wait_ge(vector_free, T * 4 + 2 * n + 2)
                        else:
                            pe.wait_ge(scalar_free, T * 4 + 2 * (n - 2) + 2)
                        m = 0
                        for k in range(KD):
                            for xs, ws in ((xT_hi, w_hi), (xT_hi, w_lo), (xT_lo, w_hi)):
                                ins = pe.matmul(main[n][:, :], xs[:, par, j, k, :], ws[:, k, n * 512:(n + 1) * 512],
                                                start=(m == 0), stop=(m == 3 * KD - 1))
                                m += 1
                        ins.then_inc(bank_done, 1)
                        if at == 1:
                            if j == 0:
                                pe.wait_ge(gT_ready, G + 1)
                            pe.wait_ge(acc_step, T + 1)
                            pe.matmul(bias_ps[:, 0:D], gT[:, :], eb_rows[:, j, :], start=True,
                                      stop=True).then_inc(bias_done, 1)

                turn(0)
                pe.wait_ge(w_ready, 1)
                gate_logits(0, 0)
                pe.wait_ge(w_loaded, 16 * (3 + TG))

                def group(G, par, left):
                    turn_gates(G)
                    experts(G, par, 0)
                    if left:
                        turn(G + 1)
                    experts(G, par, 1)
                    if left:
                        gate_logits(G + 1, 1 - par)
                    experts(G, par, 2)
                    experts(G, par, 3)

                pipelined(pe, group)


class Shared:
    pass


def bass_program(nc, x, q_wT, k_wT, v_wT, o_wT, dw_r, pw_rT, dw_i, pw_iT, a_gate_wT, alpha_raw, w_in, b_in, w_out, b_out,
                 rel_emb, gate_wT, gate_b, expert_w, expert_b, dft, idft_high, idft_low, mask, out):
    C = Shared()
    B, S, D = x.shape
    C.B, C.S, C.D = B, S, D
    C.NT = B * S // P
    C.CH, C.LOW, C.TAPS = 64, 4, dw_r.shape[2]
    C.NRE, C.NIM = C.CH // 2 + 1 - C.LOW, C.CH // 2 - C.LOW
    C.HD, C.NKV = 64, k_wT.shape[1] // 64
    C.q_wT, C.k_wT, C.v_wT, C.o_wT, C.a_gate_wT, C.alpha_raw = q_wT, k_wT, v_wT, o_wT, a_gate_wT, alpha_raw
    C.dw, C.pwT = (dw_r, dw_i), (pw_rT, pw_iT)
    C.dft, C.idft_high, C.idft_low, C.mask = dft, idft_high, idft_low, mask
    C.H = rel_emb.shape[1]
    C.w_in, C.b_in, C.w_out, C.b_out, C.rel_emb = w_in, b_in, w_out, b_out, rel_emb
    C.E, C.TG = gate_b.shape[0], 4
    C.gate_wT, C.gate_b, C.expert_w, C.expert_b = gate_wT, gate_b, expert_w, expert_b

    C.x_rows = x.flatten_outer_dims().rearrange("(t p) d -> p t d", p=P)
    out_rows = out.flatten_outer_dims().rearrange("(t p) d -> p t d", p=P)
    with ExitStack() as ctx:
        C.xres = ctx.enter_context(nc.sbuf_tensor("xres", [P, C.NT, D], F32))
        C.ident = ctx.enter_context(nc.sbuf_tensor("ident", [P, P], F32))
        C.vector_passed = ctx.enter_context(nc.semaphore("vector_passed"))
        C.pool_passed = ctx.enter_context(nc.semaphore("pool_passed"))
        spectral_layer(nc, C)
        with ExitStack() as weights:
            load_position = position_weights(nc, C, weights)
            token_ffn(nc, C, "_f1", None, load_position)
            position_attention(nc, C)
        token_ffn(nc, C, "_f2", out_rows)


_A, _B, _F = 'L0_attn_a_', 'L0_attn_b_', 'L0_ffn_'
_INS = [('x', _A + 'hidden_states', None), ('qw', _A + 'q_w', (1, 0)), ('kw', _A + 'k_w', (1, 0)), ('vw', _A + 'v_w', (1, 0)),
        ('ow', _A + 'o_w', (1, 0)), ('dwr', _A + 'dw_r', None), ('pwr', _A + 'pw_r', (1, 0)), ('dwi', _A + 'dw_i', None),
        ('pwi', _A + 'pw_i', (1, 0)), ('agw', _A + 'gate_w', (1, 0)), ('alpha', _A + 'alpha_raw', None),
        ('w_in', _B + 'W_in', None), ('b_in', _B + 'b_in', None), ('w_out', _B + 'W_out', None), ('b_out', _B + 'b_out', None),
        ('rel_emb', _B + 'rel_emb', None),
        ('fgw', _F + 'gate_w', (1, 0)), ('fgb', _F + 'gate_b', None), ('few', _F + 'expert_w', (1, 0, 2)),
        ('feb', _F + 'expert_b', None),
        ('dft', None, None), ('idh', None, None), ('idl', None, None), ('mask', None, None)]
_OUTS = [((16, 512, 256), 'float32')]


def fourier_constants():
    import numpy as _np

    CH, LOW, ROWS = 64, 4, 128
    n = _np.arange(CH)[:, None]
    k = _np.arange(CH // 2 + 1)[None, :]
    ang = 2 * _np.pi * ((n * k) % CH) / CH
    fwd_re, fwd_im = _np.cos(ang), -_np.sin(ang)
    fwd_im[:, 0] = fwd_im[:, CH // 2] = 0.0
    weight = _np.where((k == 0) | (k == CH // 2), 1.0, 2.0) / CH
    inv_re, inv_im = (fwd_re * weight).T, (fwd_im * weight).T
    NRE, NIM = CH // 2 + 1 - LOW, CH // 2 - LOW
    dft = _np.zeros((ROWS, 4 * LOW + 2 * (NRE + NIM)))
    high = _np.zeros((ROWS, ROWS))
    low = _np.zeros((8, ROWS, ROWS))
    for c in range(2):
        t = slice(CH * c, CH * (c + 1))
        dft[t, LOW * c:LOW * (c + 1)] = fwd_re[:, :LOW]
        dft[t, LOW * (2 + c):LOW * (3 + c)] = fwd_im[:, :LOW]
        re0, im0 = c * NRE, 2 * NRE + c * NIM
        dft[t, 4 * LOW + re0:4 * LOW + re0 + NRE] = fwd_re[:, LOW:]
        dft[t, 4 * LOW + im0:4 * LOW + im0 + NIM] = fwd_im[:, LOW:CH // 2]
        high[re0:re0 + NRE, t] = inv_re[LOW:]
        high[im0:im0 + NIM, t] = inv_im[LOW:CH // 2]
        for tile in range(8):
            r = 64 * (tile // 4) + LOW * (2 * (tile % 4) + c)
            low[tile, r:r + LOW, t] = inv_re[:LOW]
            low[tile, r + 32:r + 32 + LOW, t] = inv_im[:LOW]
    row = _np.arange(ROWS)
    seq, chunk = row // 32, row % 32 // LOW
    barred = (seq[:, None] != seq[None, :]) | (chunk[:, None] < chunk[None, :])
    mask = _np.where(barred, 1e30, 0.0)
    return {"dft": dft, "idh": high, "idl": low, "mask": mask}
_OUTS = [((16, 512, 256), 'float32')]


def kernel(**inputs):
    import numpy as _np
    import concourse.bacc as _bacc
    from concourse import mybir as _mybir
    from concourse.bass_utils import run_bass_kernel_spmd as _run

    nc = _bacc.Bacc("TRN2", target_bir_lowering=False, num_devices=1)
    arrays, args, constants = {}, [], fourier_constants()
    for name, source, axes in _INS:
        a = _np.asarray(inputs[source]) if source else constants[name].astype(_np.float32)
        a = _np.ascontiguousarray(a if axes is None else a.transpose(axes))
        arrays[f"in_{name}_dram"] = a
        args.append(nc.dram_tensor(f"in_{name}_dram", a.shape, _mybir.dt.from_np(a.dtype), kind="ExternalInput").ap())
    for i, (shape, dtype) in enumerate(_OUTS):
        dt = _mybir.dt.from_np(_np.dtype(dtype))
        args.append(nc.dram_tensor(f"out_{i}_dram", shape, dt, kind="ExternalOutput").ap())
    bass_program(nc, *args)
    r = _run(nc, [arrays], core_ids=[0])
    got = tuple(r.results[0][f"out_{i}_dram"] for i in range(len(_OUTS)))
    return got[0]
```
